# Optimizing a Trainium2 kernel written in Bass

```python
import numpy as np
import jax
import jax.numpy as jnp

def _softmax(x, axis=-1):
    return jax.nn.softmax(x, axis=axis)

def _gelu(x):
    return jax.nn.gelu(x, approximate=True)

def _silu(x):
    return jax.nn.silu(x)

def _sigmoid(x):
    return jax.nn.sigmoid(x)

def _layernorm(x, axis=-1, eps=1e-05):
    m = jnp.mean(x, axis=axis, keepdims=True)
    v = jnp.var(x, axis=axis, keepdims=True)
    return (x - m) / jnp.sqrt(v + eps)

def _scatter_add(tgt, idx, src, axis=0):
    return tgt.at[idx].add(src)

def _segment_sum(src, seg, n):
    return jax.ops.segment_sum(src, seg, n)
kernel_name = 'mk_xattn_seq_d1_seqx_r2_3674f1'

def setup_inputs(seed: int=0):
    np.random.seed(seed)
    _w = jnp.asarray

    def _rec_inputs():
        import jax
        import jax.numpy as jnp
        _rk = jax.random.key(seed)
        x = 7.22e-05 + 1 * jax.random.normal(jax.random.fold_in(_rk, 1), (16, 256, 2048), jnp.float32)
        _lenS = 256 - jax.random.randint(jax.random.fold_in(_rk, 7), (16,), 0, max(1, 256 // 4) + 1, jnp.int32)
        _lenS2 = 256 - jax.random.randint(jax.random.fold_in(_rk, 8), (16,), 0, max(1, 256 // 4) + 1, jnp.int32)
        _ctx_4096P = jax.random.normal(jax.random.fold_in(_rk, 11), (16, 16, 2048), jnp.float32)
        _ctx_4096c = jax.random.dirichlet(jax.random.fold_in(_rk, 511), 0.3 * jnp.ones((16,), jnp.float32), (16, 256))
        _ctx_4096t = jnp.einsum('bsk,bkd->bsd', _ctx_4096c, _ctx_4096P)
        _ctx_4096t = _ctx_4096t * jax.lax.rsqrt(jnp.mean(jnp.square(_ctx_4096t)) + 1e-12) * 0.953939
        ctx_4096 = 4.13588e-05 + 0.999923 * (_ctx_4096t + 0.3 * jax.random.normal(jax.random.fold_in(_rk, 611), (16, 256, 2048), jnp.float32))
        _validS = jnp.arange(256)[None, :] < _lenS[:, None]
        _validS2 = jnp.arange(256)[None, :] < _lenS2[:, None]
        _causal = jnp.tril(jnp.ones((256, 256), dtype=bool))
        mask_Bx1x4096_ff1 = jnp.where(jnp.ones((16, 1, 2048), dtype=bool), 1.0, 0.0).astype(jnp.float32)
        return (x, ctx_4096, mask_Bx1x4096_ff1)
    x, ctx_4096, mask_Bx1x4096_ff1 = _rec_inputs()

    def _L0_xattn_setup():
        import jax, jax.numpy as jnp
        import numpy as np
        NUM_HEADS = 8
        CHUNK = 64
        EPS = 1e-05
        NEG = -1000000000.0

        def _chunk_attn(q, k, v, masks, W_in, b_in, W_out, b_out):
            N, C, T = q.shape
            H, Dh = (NUM_HEADS, C // NUM_HEADS)
            nc = T // CHUNK
            Wq, Wk, Wv = jnp.split(W_in, 3, axis=0)
            bq, bk, bv = jnp.split(b_in, 3, axis=0)

            def proj(t, W, b):
                t = t.transpose(0, 2, 1) @ W.T + b
                return t.reshape(N, nc, CHUNK, H, Dh)
            qh = proj(q, Wq, bq)
            kh = proj(k, Wk, bk)
            vh = proj(v, Wv, bv)
            scale = 1.0 / jnp.sqrt(jnp.asarray(Dh, q.dtype))
            scores = jnp.einsum('bnqhd,bnkhd->bnhqk', qh, kh) * scale
            km = masks[:, 0, :].reshape(N, nc, CHUNK)
            scores = scores + jnp.where(km[:, :, None, None, :] > 0, 0.0, NEG)
            attn = jax.nn.softmax(scores, axis=-1)
            out = jnp.einsum('bnhqk,bnkhd->bnqhd', attn, vh).reshape(N, T, C)
            out = out @ W_out.T + b_out
            out = out.transpose(0, 2, 1) * masks
            return out
        key = jax.random.key(seed)
        ks = jax.random.split(key, 8)
        N, C, T = (4, 256, 2048)
        x = jax.random.normal(ks[0], (N, C, T), dtype=jnp.float32)
        q = jax.random.normal(ks[1], (N, C, T), dtype=jnp.float32)
        k = jax.random.normal(ks[2], (N, C, T), dtype=jnp.float32)
        v = jax.random.normal(ks[3], (N, C, T), dtype=jnp.float32)
        masks = jnp.ones((N, 1, T), dtype=jnp.float32)
        s = 1.0 / np.sqrt(C)
        W_in = jax.random.normal(ks[4], (3 * C, C), dtype=jnp.float32) * s
        b_in = jnp.zeros((3 * C,), dtype=jnp.float32)
        W_out = jax.random.normal(ks[5], (C, C), dtype=jnp.float32) * s
        b_out = jnp.zeros((C,), dtype=jnp.float32)
        return {'x': x, 'q': q, 'k': k, 'v': v, 'masks': masks, 'W_in': W_in, 'b_in': b_in, 'W_out': W_out, 'b_out': b_out}
    _L0_xattn_all = _L0_xattn_setup()
    _L0_xattn_in = {k: v for k, v in _L0_xattn_all.items() if k in ('W_in', 'b_in', 'W_out', 'b_out')}
    del _L0_xattn_all
    return {'x': x, 'ctx_4096': ctx_4096, 'mask_Bx1x4096_ff1': mask_Bx1x4096_ff1, 'L0_xattn_W_in': _L0_xattn_in['W_in'], 'L0_xattn_b_in': _L0_xattn_in['b_in'], 'L0_xattn_W_out': _L0_xattn_in['W_out'], 'L0_xattn_b_out': _L0_xattn_in['b_out']}

def reference(x, ctx_4096, mask_Bx1x4096_ff1, L0_xattn_W_in, L0_xattn_b_in, L0_xattn_W_out, L0_xattn_b_out):
    import jax
    import jax.numpy as jnp

    def _L0_xattn_ref(x, q, k, v, masks, W_in, b_in, W_out, b_out):
        import jax, jax.numpy as jnp
        import numpy as np
        NUM_HEADS = 8
        CHUNK = 64
        EPS = 1e-05
        NEG = -1000000000.0

        def _chunk_attn(q, k, v, masks, W_in, b_in, W_out, b_out):
            N, C, T = q.shape
            H, Dh = (NUM_HEADS, C // NUM_HEADS)
            nc = T // CHUNK
            Wq, Wk, Wv = jnp.split(W_in, 3, axis=0)
            bq, bk, bv = jnp.split(b_in, 3, axis=0)

            def proj(t, W, b):
                t = t.transpose(0, 2, 1) @ W.T + b
                return t.reshape(N, nc, CHUNK, H, Dh)
            qh = proj(q, Wq, bq)
            kh = proj(k, Wk, bk)
            vh = proj(v, Wv, bv)
            scale = 1.0 / jnp.sqrt(jnp.asarray(Dh, q.dtype))
            scores = jnp.einsum('bnqhd,bnkhd->bnhqk', qh, kh) * scale
            km = masks[:, 0, :].reshape(N, nc, CHUNK)
            scores = scores + jnp.where(km[:, :, None, None, :] > 0, 0.0, NEG)
            attn = jax.nn.softmax(scores, axis=-1)
            out = jnp.einsum('bnhqk,bnkhd->bnqhd', attn, vh).reshape(N, T, C)
            out = out @ W_out.T + b_out
            out = out.transpose(0, 2, 1) * masks
            return out
        out = _chunk_attn(q, k, v, masks, W_in, b_in, W_out, b_out) + x
        mu = jnp.mean(out, axis=2, keepdims=True)
        var = jnp.mean(jnp.square(out - mu), axis=2, keepdims=True)
        return (out - mu) * jax.lax.rsqrt(var + EPS)
    x = _L0_xattn_ref(x, ctx_4096, ctx_4096, ctx_4096, mask_Bx1x4096_ff1, L0_xattn_W_in, L0_xattn_b_in, L0_xattn_W_out, L0_xattn_b_out)
    return x

_drawn_inputs = setup_inputs


def setup_inputs(seed=0):
    import zlib

    import numpy as np

    out = dict(_drawn_inputs(seed))
    spreads = {'L0_xattn_b_in': (0.0, 0.476), 'L0_xattn_b_out': (0.0, 0.8)}
    factors = {}
    for name, (base, spread) in spreads.items():
        noise = np.random.default_rng([zlib.crc32(name.encode()), seed]).standard_normal(out[name].shape)
        drawn = base * np.exp(spread * noise) if base else spread * noise
        out[name] = jnp.asarray(drawn.astype(out[name].dtype))
    for name, factor in factors.items():
        out[name] = (out[name] * factor).astype(out[name].dtype)
    return out
```

```python
from contextlib import ExitStack

import concourse.bass as bass
from concourse import mybir

F32 = mybir.dt.float32
F32R = mybir.dt.float32r
F16 = mybir.dt.float16
BF16 = mybir.dt.bfloat16
ALU = mybir.AluOpType
ACT = mybir.ActivationFunctionType
AX = mybir.AxisListType

P = 128
N, C, T = 16, 256, 2048
HEADS, CHUNK = 8, 64
DH = C // HEADS
G = C // P
UNIT = 512
STEP = 128
UB = T // UNIT
SB = T // STEP
SU = UNIT // STEP
CU = UNIT // CHUNK
UNITS, STEPS = N * UB, N * SB
HI, LO = 0, 1
EPS = 1e-5
NEG = -1e9
SCALE = 1.0 / DH ** 0.5
NEG_PARTS = (-998244352.0, -1753088.0, -2560.0)

FIRST = -12
LOOP_AT = 24
LOOPS = N - 3
LAST = STEPS + 13


class At:

    def __init__(self, b, i):
        self.b, self.i = b, i
        self.fixed = isinstance(b, int)

    def item(self, lag, period, per_batch, total):
        i = self.i - lag
        if i % period:
            return None
        n = i // period
        if self.fixed:
            return n if 0 <= self.b * per_batch + n < total else None
        assert 0 <= n and (LOOPS - 1) * per_batch + n < total
        return n

    def count(self, per_batch, n):
        return self.b * per_batch + n


def wait(eng, at, sem, per_batch, n, times=1):
    value = at.b * (per_batch * times) + n * times
    if at.fixed and value <= 0:
        return
    assert at.fixed or n > 0
    eng.wait_ge(sem, value)


def wait_all(eng, at, waits, registers):
    values = [(sem, at.b * (per_batch * times) + n * times) for sem, per_batch, n, times in waits]
    if at.fixed:
        values = [(sem, value) for sem, value in values if value > 0]
    else:
        assert all(n > 0 for _, _, n, _ in waits)
        for (sem, value), register in zip(values, registers):
            eng.reg_mov(register, value)
        values = [(sem, register) for (sem, _), register in zip(values, registers)]
    for sem, value in values:
        eng.wait_ge(sem, value)


def all_steps(eng, step):
    for i in range(FIRST, LOOP_AT):
        step(At(0, i))
    with eng.Fori(0, LOOPS) as b:
        for i in range(LOOP_AT, LOOP_AT + SB):
            step(At(b, i))
    for i in range(LOOP_AT, LAST - LOOPS * SB):
        step(At(LOOPS, i))


def build(nc, x, ctx_in, masks, w_in, b_in, w_out, b_out, out):
    es = ExitStack()
    with es:
        def sb(name, shape, dt):
            return es.enter_context(nc.sbuf_tensor(name, shape, dt))

        def sem(name):
            return es.enter_context(nc.semaphore(name))

        es.enter_context(nc.allow_non_contiguous_dma(reason="bias vectors, once"))

        w_rows = sb("w_rows", [P, 3 * G, C], F32)
        wo_rows = sb("wo_rows", [P, G, C], F32)
        w_t = sb("w_t", [P, 4 * G * G, P], F32)
        w_hi = sb("w_hi", [P, 4 * G * G, P], F32R)
        w_lo = sb("w_lo", [P, 4 * G * G, P], F32R)
        b_in_col = sb("b_in_col", [P, 3 * G], F32)
        b_out_col = sb("b_out_col", [P, G], F32)
        q_bias = sb("q_bias", [P, G], F32)
        y_bias = sb("y_bias", [P, G], F32)
        ident = sb("ident", [P, P], F32)
        neg_w = sb("neg_w", [P, P], BF16)
        minus_half, minus_one, eps = (sb(name, [P, G], F32) for name in ("minus_half", "minus_one", "eps"))

        ctx_raw = [sb(f"ctx_raw{i}", [P, G, UNIT], F32) for i in range(2)]
        ctx_hi = [sb(f"ctx_hi{i}", [P, G, UNIT], F32R) for i in range(2)]
        ctx_lo = [sb(f"ctx_lo{i}", [P, G, UNIT], F32R) for i in range(2)]
        x_sb = [sb(f"x_sb{i}", [P, G, UNIT], F32) for i in range(2)]
        mask = [sb(f"mask{i}", [P, UNIT], F32) for i in range(4)]
        masked = [sb(f"masked{i}", [P, UNIT], BF16) for i in range(2)]
        q_sb = [sb(f"q_sb{i}", [P, 2, G, CU, 2 * CHUNK], F16) for i in range(2)]
        k_dense = [sb(f"k_dense{g}", [P, 2, UNIT], F16) for g in range(G)]
        k_sb = [sb(f"k_sb{i}", [P, G, 2, 2, UNIT], F16) for i in range(2)]
        v_sb = [sb(f"v_sb{i}", [P, 2, CU, 4 * 2 * CHUNK], F16) for i in range(2)]
        row_max = [sb(f"row_max{i}", [P, 8], F32) for i in range(2)]
        row_sum = [sb(f"row_sum{i}", [P, 8], F32) for i in range(2)]
        row_inv = [sb(f"row_inv{i}", [P, 8], F32) for i in range(4)]
        probs = [sb(f"probs{i}", [P, 4 * P], F32) for i in range(4)]
        pt_hi = [sb(f"pt_hi{i}", [P, 4 * P], F16) for i in range(2)]
        pt_lo = [sb(f"pt_lo{i}", [P, 4 * P], F16) for i in range(2)]
        o_hi = [sb(f"o_hi{i}", [P, G, UNIT], F32R) for i in range(2)]
        o_lo = [sb(f"o_lo{i}", [P, G, UNIT], F32R) for i in range(2)]
        y_sb = [sb(f"y_sb{i}", [P, UNIT], F32) for i in range(2)]
        z_sb = sb("z_sb", [P, UB, G, UNIT], F32)
        stats = sb("stats", [P, G, UB, 6], F32)
        mean_var = sb("mean_var", [P, G, 2], F32)
        var_eps = sb("var_eps", [P, G], F32)
        rstd = sb("rstd", [P, G], F32)
        shift = sb("shift", [P, G], F32)
        out_sb = [sb(f"out_sb{i}", [P, UNIT], F32) for i in range(4)]

        def bank(name):
            return es.enter_context(nc.psum_tensor(name, [P, UNIT], F32))

        qk_bank = bank("qk_bank")
        vy_bank = bank("vy_bank")
        s_bank = [bank(f"s_bank{i}") for i in range(2)]
        t_bank = [bank(f"t_bank{i}") for i in range(2)]
        o_bank = [bank(f"o_bank{i}") for i in range(2)]

        w_loaded, consts_ready, w_turned, w_copied, w_split, w_hi_done = (
            sem("w_loaded"), sem("consts_ready"), sem("w_turned"), sem("w_copied"), sem("w_split"), sem("w_hi_done"))
        q_bias_ready, y_bias_psum, y_bias_ready = sem("q_bias_ready"), sem("y_bias_psum"), sem("y_bias_ready")
        ident_zeroed, neg_zeroed = sem("ident_zeroed"), sem("neg_zeroed")
        q_zeroed, k_zeroed, v_zeroed = sem("q_zeroed"), sem("k_zeroed"), sem("v_zeroed")
        ctx_loaded = [sem(f"ctx_loaded{i}") for i in range(2)]
        x_loaded = [sem(f"x_loaded{i}") for i in range(2)]
        mask_loaded = [sem(f"mask_loaded{i}") for i in range(4)]
        k_spread = [sem(f"k_spread{i}") for i in range(2)]
        out_free = [sem(f"out_free{i}") for i in range(4)]
        ctx_hi_done, ctx_lo_done, masked_done = sem("ctx_hi_done"), sem("ctx_lo_done"), sem("masked_done")
        qk_proj, qk_hi_done, qk_lo_done = sem("qk_proj"), sem("qk_hi_done"), sem("qk_lo_done")
        v_proj, v_hi_done, v_lo_done = sem("v_proj"), sem("v_hi_done"), sem("v_lo_done")
        scored, max_done, shifted, exp_done = sem("scored"), sem("max_done"), sem("shifted"), sem("exp_done")
        sum_done, inv_done, normed = sem("sum_done"), sem("inv_done"), sem("normed")
        turned, pt_hi_done, pt_lo_done = sem("turned"), sem("pt_hi_done"), sem("pt_lo_done")
        attended, o_hi_done, o_lo_done = sem("attended"), sem("o_hi_done"), sem("o_lo_done")
        y_proj, y_masked, z_done = sem("y_proj"), sem("y_masked"), sem("z_done")
        aggregated, rstd_chain, rstd_done = sem("aggregated"), sem("rstd_chain"), sem("rstd_done")
        out_done = sem("out_done")

        def w_block(matrix, co, ci):
            return (matrix * G + co) * G + ci

        def scores_of(at):
            return at.item(0, 1, SB, STEPS)

        def attend_of(at):
            return at.item(2, 1, SB, STEPS)

        def qk_of(at):
            return at.item(-5, 1, SB, UNITS * 4)

        def v_proj_of(at):
            return at.item(-2, 2, SB // 2, UNITS * 2)

        def v_evac_of(at):
            return at.item(-1, 2, SB // 2, UNITS * 2)

        def y_proj_of(at):
            return at.item(7, 2, SB // 2, UNITS * G)

        def y_evac_of(at):
            return at.item(8, 2, SB // 2, UNITS * G)

        def stats_of(at):
            return at.item(9, 2, SB // 2, UNITS * G)

        def o_evac_of(at):
            return at.item(4, 2, SB // 2, UNITS * 2)

        def ctx_load_of(at):
            return at.item(-12, 4, UB, UNITS)

        def ctx_split_of(at, ci):
            return at.item(-7 + ci, 4, UB, UNITS)

        def mask_load_of(at):
            return at.item(-5, 4, UB, UNITS)

        def masked_of(at):
            return at.item(-2, 4, UB, UNITS)

        def x_load_of(at):
            return at.item(3, 4, UB, UNITS)

        def rstd_of(at):
            return at.item(23, SB, 1, N)

        def out_of(at):
            for v in range(UB):
                n = at.item(24 + v, SB, 1, N)
                if n is not None:
                    return n, v
            return None

        def o_tile(h):
            return o_bank[h % 2][:, :].rearrange("p (g t) -> p g t", g=G)

        def v_moves(v, half, part):
            moves = []
            psum = vy_bank[:, :].rearrange("p (a h s d) -> p a h s d", h=2 * G, s=2, d=DH)
            chunks = v_sb[v % 2][:, part, :, :].rearrange("p (a b) (h w) -> p a b h w", b=2, w=2 * CHUNK)
            for ab in range(2):
                for slot in range(2):
                    dst = chunks[64 * slot:64 * slot + 64, 2 * half:2 * half + 2, ab, :, DH * slot:DH * slot + DH]
                    moves.append((dst, psum[64 * ab:64 * ab + 64, :, :, slot, :]))
            return [(k == 3, m) for k, m in enumerate(moves)]

        block = es.enter_context(nc.Block())

        @block.sync
        def _(sp):
            sp.dma_start(w_rows[:, :, :], w_in.rearrange("(t p) c -> p t c", p=P)).then_inc(w_loaded, 16)
            sp.dma_start(wo_rows[:, :, :], w_out.rearrange("(t p) c -> p t c", p=P)).then_inc(w_loaded, 16)
            sp.dma_start(b_in_col[:, :], b_in.rearrange("(t p) -> p t", p=P)).then_inc(w_loaded, 16)
            sp.dma_start(b_out_col[:, :], b_out.rearrange("(t p) -> p t", p=P)).then_inc(w_loaded, 16)
            ctx_v = ctx_in.rearrange("n (g p) t -> n p g t", p=P)
            x_v = x.rearrange("n (g p) t -> n p g t", p=P)
            out_v = out.rearrange("n (g p) t -> n g p t", p=P)

            def tokens(v):
                t0 = v % UB * UNIT
                return slice(t0, t0 + UNIT)

            registers = [sp.alloc_register(f"wait{k}") for k in range(5)]

            def step(at):
                spread, waits = None, []
                j = qk_of(at)
                if j is not None and j % 4 < G:
                    spread = v, g = j // 4, j % 4
                    if at.fixed and at.b == 0 and v < 2 and g == 0:
                        sp.wait_ge(k_zeroed, v + 1)
                    waits += [(qk_lo_done, SB, j + 1, 1), (scored, SB, (v - 1) * SU, 1)]
                v_ctx, v_mask, v_x = ctx_load_of(at), mask_load_of(at), x_load_of(at)
                if v_ctx is not None:
                    waits.append((ctx_lo_done, UB * G, (v_ctx - 1) * G, 1))
                if v_mask is not None:
                    waits.append((y_masked, UB * G, (v_mask - 3) * G, 1))
                if v_x is not None:
                    waits.append((z_done, UB * G, (v_x - 1) * G, 1))
                wait_all(sp, at, waits, registers)
                if spread is not None:
                    v, g = spread
                    for quad in range(4):
                        rows = slice(DH * quad, DH * (quad + 1))
                        sp.dma_start(k_sb[v % 2][rows, g, :, quad % 2, :], k_dense[g][rows, :, :]) \
                          .then_inc(k_spread[v % 2], 16)
                if v_ctx is not None:
                    v = v_ctx
                    sp.dma_start(ctx_raw[v % 2][:, :, :], ctx_v[at.b + v // UB, :, :, tokens(v)]) \
                      .then_inc(ctx_loaded[v % 2], 16)
                if v_mask is not None:
                    v = v_mask
                    row = masks[at.b + v // UB, :, tokens(v)]
                    sp.dma_start(mask[v % 4][:, :], row.to_broadcast([P, UNIT])).then_inc(mask_loaded[v % 4], 16)
                if v_x is not None:
                    v = v_x
                    sp.dma_start(x_sb[v % 2][:, :, :], x_v[at.b + v // UB, :, :, tokens(v)]) \
                      .then_inc(x_loaded[v % 2], 16)
                bv = out_of(at)
                if bv is not None:
                    n, v = bv
                    for g in range(G):
                        m = v * G + g
                        wait(sp, at, out_done, UB * G, n * UB * G + m + 1)
                        sp.dma_start(out_v[at.b + n, g, :, tokens(v)], out_sb[m % 4][:, :]) \
                          .then_inc(out_free[m % 4], 16)

            all_steps(sp, step)
            for s in out_free:
                sp.wait_ge(s, 16 * N * UB * G // 4 + 16)

        @block.gpsimd
        def _(pool):
            pool.memset(ident[:, :], 0.0).then_inc(ident_zeroed, 1)
            for tile, value in ((minus_half, -0.5), (minus_one, -1.0), (eps, EPS)):
                pool.memset(tile[:, :], value).then_inc(consts_ready, 1)
            pool.wait_ge(ident_zeroed, 1)
            pool.affine_select(out=ident[:, :], in_=ident[:, :], compare_op=ALU.not_equal, fill=1.0, base=0,
                               pattern=[[-1, P]], channel_multiplier=1).then_inc(consts_ready, 1)
            for i in range(2):
                pool.memset(k_sb[i][:, :, :, :, :].bitcast(F32), 0.0).then_inc(k_zeroed, 1)

            def step(at):
                r = scores_of(at)
                if r is not None:
                    wait(pool, at, inv_done, SB, r + 1)
                    p3 = probs[r % 4][:, :].rearrange("p (a k) -> p a k", k=CHUNK)
                    inv = row_inv[r % 4][:, :].unsqueeze(2).to_broadcast([P, 8, CHUNK])
                    pool.tensor_tensor(p3, p3, inv, ALU.mult).then_inc(normed, 1)
                y = y_evac_of(at)
                if y is not None:
                    v, g = y // G, y % G
                    wait(pool, at, y_masked, UB * G, y + 1)
                    if g == 0:
                        wait(pool, at, x_loaded[v % 2], UB // 2, v // 2 + 1, 16)
                    wait(pool, at, out_done, UB * G, y - UB * G + 1)
                    pool.tensor_tensor(z_sb[:, v % UB, g, :], y_sb[y % 2][:, :], x_sb[v % 2][:, g, :], ALU.add) \
                        .then_inc(z_done, 1)
                for ci in range(G):
                    v = ctx_split_of(at, ci)
                    if v is not None:
                        wait(pool, at, ctx_hi_done, UB, v + 1)
                        pool.tensor_tensor(ctx_lo[v % 2][:, ci, :], ctx_raw[v % 2][:, ci, :],
                                           ctx_hi[v % 2][:, ci, :].bitcast(F32), ALU.subtract).then_inc(ctx_lo_done, 1)
                n = rstd_of(at)
                if n is not None:
                    wait(pool, at, aggregated, 1, n + 1)
                    wait(pool, at, out_done, UB * G, n * UB * G)
                    pool.tensor_tensor(var_eps[:, :], mean_var[:, :, 1], eps[:, :], ALU.add).then_inc(rstd_chain, 1)
                    wait(pool, at, rstd_chain, 1, n + 1)
                    pool.tensor_tensor(rstd[:, :], var_eps[:, :], minus_half[:, :], ALU.pow).then_inc(rstd_done, 1)
                    wait(pool, at, rstd_done, 3, 3 * n + 1)
                    pool.tensor_tensor(shift[:, :], mean_var[:, :, 0], rstd[:, :], ALU.mult).then_inc(rstd_done, 1)
                    wait(pool, at, rstd_done, 3, 3 * n + 2)
                    pool.tensor_tensor(shift[:, :], shift[:, :], minus_one[:, :], ALU.mult).then_inc(rstd_done, 1)

            pool.wait_ge(k_zeroed, 2)
            all_steps(pool, step)

        @block.scalar
        def _(act):
            for s in out_free:
                act.sem_inc(s, 16)
            act.wait_ge(w_loaded, 64)
            nc.scalar.mul(q_bias[:, :], b_in_col[:, 0:G], SCALE).then_inc(q_bias_ready, 1)
            for m in range(4):
                act.wait_ge(w_turned, m + 1)
                src = (s_bank + t_bank)[m]
                nc.scalar.activation(w_t[:, 4 * m:4 * m + 4, :], src[:, :].rearrange("p (a c) -> p a c", c=P), ACT.Copy,
                                     scale=SCALE if m == 0 else 1.0).then_inc(w_copied, 1)
                act.wait_ge(w_copied, m + 1)
                nc.scalar.activation(w_hi[:, 4 * m:4 * m + 4, :], w_t[:, 4 * m:4 * m + 4, :], ACT.Copy) \
                    .then_inc(w_hi_done, 1)
            act.wait_ge(q_bias_ready, 1)

            def step(at):
                w = v_evac_of(at)
                if w is not None:
                    v, half = w // 2, w % 2
                    if at.fixed and at.b == 0 and v < 2 and half == 0:
                        act.wait_ge(v_zeroed, v + 1)
                    wait(act, at, v_proj, SB // 2, w + 1)
                    wait(act, at, attended, SB, 2 * (w - 4) + 2)
                    for last, (dst, src) in v_moves(v, half, HI):
                        ins = nc.scalar.activation(dst, src, ACT.Copy)
                        if last:
                            ins.then_inc(v_hi_done, 1)
                bv = out_of(at)
                if bv is not None:
                    n, v = bv
                    wait(act, at, rstd_done, 3, 3 * n + 3)
                    for g in range(G):
                        m = v * G + g
                        wait(act, at, out_free[m % 4], 2, 2 * n + m // 4 + 1, 16)
                        nc.scalar.activation(out_sb[m % 4][:, :], z_sb[:, v, g, :], ACT.Identity,
                                             bias=shift[:, g:g + 1], scale=rstd[:, g:g + 1]).then_inc(out_done, 1)
                h = o_evac_of(at)
                if h is not None:
                    v, half = h // 2, h % 2
                    wait(act, at, attended, SB, 2 * h + 2)
                    wait(act, at, y_proj, UB * G, (v - 1) * G)
                    nc.scalar.activation(o_hi[v % 2][:, :, 256 * half:256 * half + 256], o_tile(h), ACT.Copy) \
                        .then_inc(o_hi_done, 1)
                r = attend_of(at)
                if r is not None:
                    wait(act, at, turned, SB, r + 1)
                    wait(act, at, attended, SB, r - 1)
                    nc.scalar.activation(pt_hi[r % 2][:, :], t_bank[r % 2][:, :], ACT.Copy).then_inc(pt_hi_done, 1)
                r = scores_of(at)
                if r is not None:
                    wait(act, at, shifted, SB, r + 1)
                    nc.scalar.activation(probs[r % 4][:, :], probs[r % 4][:, :], ACT.Exp).then_inc(exp_done, 1)
                j = qk_of(at)
                if j is not None:
                    v, g = j // 4, j % 2
                    wait(act, at, qk_proj, SB, j + 1)
                    if j % 4 < G:
                        wait(act, at, k_spread[(v - 1) % 2], UB // 2, (v + 1) // 2, 16 * 4 * G)
                        nc.scalar.activation(k_dense[g][:, HI, :], qk_bank[:, :], ACT.Identity,
                                             bias=b_in_col[:, G + g:G + g + 1]).then_inc(qk_hi_done, 1)
                    else:
                        if at.fixed and at.b == 0 and v < 2 and g == 0:
                            act.wait_ge(q_zeroed, v + 1)
                        wait(act, at, scored, SB, (v - 1) * SU)
                        for up in range(2):
                            rows, cols = slice(64 * up, 64 * up + 64), slice(CHUNK * up, CHUNK * up + CHUNK)
                            ins = nc.scalar.activation(
                                q_sb[v % 2][rows, HI, g, :, cols],
                                qk_bank[rows, :].rearrange("p (c t) -> p c t", t=CHUNK), ACT.Identity,
                                bias=q_bias[rows, g:g + 1])
                        ins.then_inc(qk_hi_done, 1)
                v = ctx_split_of(at, 0)
                if v is not None:
                    wait(act, at, ctx_loaded[v % 2], UB // 2, v // 2 + 1, 16)
                    wait(act, at, v_proj, SB // 2, 2 * (v - 1))
                    nc.scalar.activation(ctx_hi[v % 2][:, :, :], ctx_raw[v % 2][:, :, :], ACT.Copy) \
                        .then_inc(ctx_hi_done, 1)

            all_steps(act, step)

        @block.vector
        def _(dve):
            dve.memset(neg_w[:, :], 0.0).then_inc(neg_zeroed, 1)
            dve.wait_ge(neg_zeroed, 1)
            for r, part in enumerate(NEG_PARTS):
                dve.memset(neg_w[32 * r:32 * r + 1, :], part).then_inc(consts_ready, 1)
            for i in range(2):
                dve.memset(q_sb[i][:, :, :, :, :].bitcast(F32), 0.0).then_inc(q_zeroed, 1)
                dve.memset(v_sb[i][:, :, :, :].bitcast(F32), 0.0).then_inc(v_zeroed, 1)
            for m in range(4):
                dve.wait_ge(w_hi_done, m + 1)
                dve.tensor_tensor(w_lo[:, 4 * m:4 * m + 4, :], w_t[:, 4 * m:4 * m + 4, :],
                                  w_hi[:, 4 * m:4 * m + 4, :].bitcast(F32), ALU.subtract).then_inc(w_split, 1)
            dve.wait_ge(y_bias_psum, 1)
            dve.tensor_tensor(y_bias[:, :], o_bank[0][:, 0:G], b_out_col[:, :], ALU.add).then_inc(y_bias_ready, 1)
            dve.wait_ge(y_bias_ready, 1)

            def step(at):
                v = masked_of(at)
                if v is not None:
                    wait(dve, at, mask_loaded[v % 4], UB // 4, v // 4 + 1, 16)
                    wait(dve, at, scored, SB, (v - 1) * SU)
                    dve.tensor_scalar(masked[v % 2][:, :], mask[v % 4][:, :], 0.0, 0.0, ALU.is_gt, ALU.is_equal) \
                       .then_inc(masked_done, 1)
                w = v_evac_of(at)
                if w is not None:
                    v, half = w // 2, w % 2
                    wait(dve, at, v_hi_done, SB // 2, w + 1)
                    for (last, (dst, src)), (_, (hi, _)) in zip(v_moves(v, half, LO), v_moves(v, half, HI)):
                        ins = dve.tensor_tensor(dst, src, hi, ALU.subtract)
                        if last:
                            ins.then_inc(v_lo_done, 1)
                y = y_evac_of(at)
                if y is not None:
                    v, g = y // G, y % G
                    wait(dve, at, y_proj, UB * G, y + 1)
                    if g == 0:
                        wait(dve, at, mask_loaded[v % 4], UB // 4, v // 4 + 1, 16)
                    wait(dve, at, z_done, UB * G, y - 1)
                    dve.scalar_tensor_tensor(out=y_sb[y % 2][:, :], in0=vy_bank[:, :], scalar=y_bias[:, g:g + 1],
                                             in1=mask[v % 4][:, :], op0=ALU.add, op1=ALU.mult).then_inc(y_masked, 1)
                h = o_evac_of(at)
                if h is not None:
                    v, cols = h // 2, slice(256 * (h % 2), 256 * (h % 2) + 256)
                    wait(dve, at, o_hi_done, SB // 2, h + 1)
                    dve.tensor_tensor(o_lo[v % 2][:, :, cols], o_tile(h), o_hi[v % 2][:, :, cols].bitcast(F32),
                                      ALU.subtract).then_inc(o_lo_done, 1)
                r = scores_of(at)
                if r is not None:
                    s3 = s_bank[r % 2][:, :].rearrange("p (a k) -> p a k", k=CHUNK)
                    p3 = probs[r % 4][:, :].rearrange("p (a k) -> p a k", k=CHUNK)
                    wait(dve, at, scored, SB, r + 1)
                    dve.tensor_reduce(row_max[r % 2][:, :], s3, AX.X, ALU.max).then_inc(max_done, 1)
                    wait(dve, at, max_done, SB, r + 1)
                    wait(dve, at, turned, SB, r - 3)
                    dve.tensor_tensor(p3, s3, row_max[r % 2][:, :].unsqueeze(2).to_broadcast([P, 8, CHUNK]),
                                      ALU.subtract).then_inc(shifted, 1)
                r = attend_of(at)
                if r is not None:
                    wait(dve, at, pt_hi_done, SB, r + 1)
                    dve.tensor_tensor(pt_lo[r % 2][:, :], t_bank[r % 2][:, :], pt_hi[r % 2][:, :], ALU.subtract) \
                       .then_inc(pt_lo_done, 1)
                r = scores_of(at)
                if r is not None:
                    p3 = probs[r % 4][:, :].rearrange("p (a k) -> p a k", k=CHUNK)
                    wait(dve, at, exp_done, SB, r + 1)
                    dve.tensor_reduce(row_sum[r % 2][:, :], p3, AX.X, ALU.add).then_inc(sum_done, 1)
                    wait(dve, at, sum_done, SB, r + 1)
                    wait(dve, at, normed, SB, r - 3)
                    dve.reciprocal(row_inv[r % 4][:, :], row_sum[r % 2][:, :]).then_inc(inv_done, 1)
                j = qk_of(at)
                if j is not None:
                    v, g = j // 4, j % 2
                    wait(dve, at, qk_hi_done, SB, j + 1)
                    if j % 4 < G:
                        dve.scalar_tensor_tensor(out=k_dense[g][:, LO, :], in0=qk_bank[:, :],
                                                 scalar=b_in_col[:, G + g:G + g + 1], in1=k_dense[g][:, HI, :],
                                                 op0=ALU.add, op1=ALU.subtract).then_inc(qk_lo_done, 1)
                    else:
                        for up in range(2):
                            rows, cols = slice(64 * up, 64 * up + 64), slice(CHUNK * up, CHUNK * up + CHUNK)
                            ins = dve.scalar_tensor_tensor(
                                out=q_sb[v % 2][rows, LO, g, :, cols],
                                in0=qk_bank[rows, :].rearrange("p (c t) -> p c t", t=CHUNK),
                                scalar=q_bias[rows, g:g + 1], in1=q_sb[v % 2][rows, HI, g, :, cols],
                                op0=ALU.add, op1=ALU.subtract)
                        ins.then_inc(qk_lo_done, 1)
                y = stats_of(at)
                if y is not None:
                    v, g = y // G, y % G
                    last = y % (UB * G) == UB * G - 1
                    wait(dve, at, z_done, UB * G, y + 1)
                    if last:
                        wait(dve, at, rstd_done, 3, 3 * (y // (UB * G)))
                    dve.bn_stats(stats[:, g, v % UB, :], z_sb[:, v % UB, g, :])
                    if last:
                        dve.drain()
                        for g in range(G):
                            ins = dve.bn_aggr(mean_var[:, g, :], stats[:, g, :, :])
                        ins.then_inc(aggregated, 1)

            all_steps(dve, step)

        @block.tensor
        def _(pe):
            pe.wait_ge(w_loaded, 64)
            pe.wait_ge(consts_ready, 4 + len(NEG_PARTS))
            for m in range(4):
                rows = w_rows if m < 3 else wo_rows
                for co in range(G):
                    for ci in range(G):
                        k = co * G + ci
                        src = rows[:, m * G + co if m < 3 else co, ci * P:(ci + 1) * P]
                        ins = nc.tensor.transpose((s_bank + t_bank)[m][:, k * P:(k + 1) * P], src, ident[:, :])
                ins.then_inc(w_turned, 1)
            pe.wait_ge(w_copied, 4)
            for co in range(G):
                for ci in range(G):
                    ins = nc.tensor.matmul(o_bank[0][:, co:co + 1], w_t[:, w_block(3, co, ci), :],
                                           b_in_col[:, 2 * G + ci:2 * G + ci + 1], start=ci == 0, stop=ci == G - 1)
            ins.then_inc(y_bias_psum, 1)
            pe.wait_ge(w_split, 4)
            pe.wait_ge(y_bias_ready, 1)

            def project(dst, matrix, co, hi, lo):
                passes = [(w, a) for w, a in ((w_hi, hi), (w_lo, hi), (w_hi, lo))]
                for k, (w, a) in enumerate(passes):
                    for ci in range(G):
                        ins = nc.tensor.matmul(dst, w[:, w_block(matrix, co, ci), :], a[:, ci, :],
                                               start=k == 0 and ci == 0, stop=k == 2 and ci == G - 1)
                return ins

            def step(at):
                r = attend_of(at)
                if r is not None:
                    wait(pe, at, normed, SB, r + 1)
                    wait(pe, at, pt_lo_done, SB, r - 1)
                    for k in range(4):
                        ins = nc.tensor.transpose(t_bank[r % 2][:, k * P:(k + 1) * P],
                                                  probs[r % 4][:, k * P:(k + 1) * P], ident[:, :])
                    ins.then_inc(turned, 1)
                r = scores_of(at)
                if r is not None:
                    v, q = r // SU, r % SU
                    if q == 0:
                        wait(pe, at, qk_lo_done, SB, 4 * v + 4)
                        wait(pe, at, k_spread[v % 2], UB // 2, v // 2 + 1, 16 * 4 * G)
                        wait(pe, at, masked_done, UB, v + 1)
                    wait(pe, at, shifted, SB, r - 1)
                    cols = masked[v % 2][:, q * STEP:(q + 1) * STEP].rearrange("p (c t) -> p c t", t=CHUNK)
                    nc.tensor.matmul(
                        s_bank[r % 2][:, :].rearrange("p (c a t) -> p c a t", c=2, t=CHUNK), neg_w[:, :],
                        cols.unsqueeze(2).to_broadcast([P, 2, 4, CHUNK]),
                        start=True, stop=False, skip_group_check=True)
                    for c in range(2):
                        chunk = 2 * q + c
                        for g in range(G):
                            dst = s_bank[r % 2][:, (c * G + g) * P:(c * G + g + 1) * P]
                            for k, (a, b) in enumerate(((HI, HI), (HI, LO), (LO, HI))):
                                ins = nc.tensor.matmul(
                                    dst, q_sb[v % 2][:, a, g, chunk, :],
                                    k_sb[v % 2][:, g, b, :, chunk * CHUNK:(chunk + 1) * CHUNK],
                                    start=False, stop=k == 2, skip_group_check=True)
                    ins.then_inc(scored, 1)
                j = qk_of(at)
                if j is not None:
                    v = j // 4
                    if j % 4 == 0:
                        wait(pe, at, ctx_lo_done, UB * G, (v + 1) * G)
                    wait(pe, at, qk_lo_done, SB, j)
                    project(qk_bank[:, :], 1 if j % 4 < G else 0, j % 2, ctx_hi[v % 2], ctx_lo[v % 2]) \
                        .then_inc(qk_proj, 1)
                w = v_proj_of(at)
                if w is not None:
                    v, half = w // 2, w % 2
                    wait(pe, at, y_masked, UB * G, w - 4)
                    for a in range(2):
                        t0 = 256 * half + P * a
                        dst = vy_bank[:, C * a:C * a + C]
                        for k, (c, m) in enumerate(((ctx_hi, w_hi), (ctx_hi, w_lo), (ctx_lo, w_hi))):
                            for ci in range(G):
                                wv = m[:, w_block(2, 0, ci):w_block(2, 1, ci) + 1:G, :]
                                ins = nc.tensor.matmul(dst.rearrange("p (a c) -> p a c", a=G),
                                                       c[v % 2][:, ci, t0:t0 + P], wv,
                                                       start=k == 0 and ci == 0, stop=k == 2 and ci == G - 1)
                    ins.then_inc(v_proj, 1)
                y = y_proj_of(at)
                if y is not None:
                    v, g = y // G, y % G
                    wait(pe, at, o_lo_done, SB // 2, 2 * v + 2)
                    if at.fixed:
                        pe.wait_ge(v_lo_done, min(at.count(SB // 2, y + 5), 2 * UNITS))
                        wait(pe, at, y_masked, UB * G, y)
                    else:
                        wait(pe, at, v_lo_done, SB // 2, y + 5)
                    project(vy_bank[:, :], 3, g, o_hi[v % 2], o_lo[v % 2]).then_inc(y_proj, 1)
                r = attend_of(at)
                if r is not None:
                    v, q = r // SU, r % SU
                    wait(pe, at, pt_lo_done, SB, r + 1)
                    if q % 2 == 0:
                        wait(pe, at, v_lo_done, SB // 2, 2 * v + q // 2 + 1)
                        wait(pe, at, o_lo_done, SB // 2, r // 2 - 1)
                    for c in range(2):
                        chunk = 2 * q + c
                        for g in range(G):
                            t0 = (q % 2) * STEP + c * CHUNK
                            dst = o_tile(r // 2)[:, g, t0:t0 + CHUNK]
                            k = 0
                            for low in range(2):
                                pcol = (c * G + g) * P + low * CHUNK
                                vcol = g * 4 * CHUNK + low * CHUNK
                                for part, pt in ((HI, pt_hi), (LO, pt_hi), (HI, pt_lo)):
                                    ins = nc.tensor.matmul(dst, v_sb[v % 2][:, part, chunk, vcol:vcol + P],
                                                           pt[r % 2][:, pcol:pcol + CHUNK],
                                                           start=k == 0, stop=k == 5)
                                    k += 1
                    ins.then_inc(attended, 1)

            all_steps(pe, step)


_INS = ['x', 'ctx_4096', 'mask_Bx1x4096_ff1', 'L0_xattn_W_in', 'L0_xattn_b_in', 'L0_xattn_W_out', 'L0_xattn_b_out']
_OUTS = [((N, C, T), 'float32')]


def kernel(**inputs):
    import numpy as _np
    import concourse.bacc as _bacc
    from concourse import mybir as _mybir
    from concourse.bass_utils import run_bass_kernel_spmd as _run

    nc = _bacc.Bacc("TRN2", target_bir_lowering=False, num_devices=1)
    arrays, args = {}, []
    for name in _INS:
        a = _np.ascontiguousarray(inputs[name])
        arrays[f"in_{name}_dram"] = a
        args.append(nc.dram_tensor(f"in_{name}_dram", a.shape, _mybir.dt.from_np(a.dtype), kind="ExternalInput").ap())
    for i, (shape, dtype) in enumerate(_OUTS):
        dt = _mybir.dt.from_np(_np.dtype(dtype))
        args.append(nc.dram_tensor(f"out_{i}_dram", shape, dt, kind="ExternalOutput").ap())
    build(nc, *args)
    r = _run(nc, [arrays], core_ids=[0])
    got = tuple(r.results[0][f"out_{i}_dram"] for i in range(len(_OUTS)))
    return got[0]
```

```python
from contextlib import ExitStack

import concourse.bass as bass
from concourse import mybir

F32 = mybir.dt.float32
F32R = mybir.dt.float32r
F16 = mybir.dt.float16
BF16 = mybir.dt.bfloat16
ALU = mybir.AluOpType
ACT = mybir.ActivationFunctionType
AX = mybir.AxisListType

P = 128
N, C, T = 16, 256, 2048
HEADS, CHUNK = 8, 64
DH = C // HEADS
G = C // P
UNIT = 512
STEP = 128
UB = T // UNIT
SB = T // STEP
SU = UNIT // STEP
CU = UNIT // CHUNK
UNITS, STEPS = N * UB, N * SB
HI, LO = 0, 1
EPS = 1e-5
NEG = -1e9
SCALE = 1.0 / DH ** 0.5
NEG_PARTS = (-998244352.0, -1753088.0, -2560.0)

FIRST = -12
LOOP_AT = 27
LOOPS = N - 3
LAST = STEPS + 15


class At:

    def __init__(self, b, i):
        self.b, self.i = b, i
        self.fixed = isinstance(b, int)

    def item(self, lag, period, per_batch, total):
        i = self.i - lag
        if i % period:
            return None
        n = i // period
        if self.fixed:
            return n if 0 <= self.b * per_batch + n < total else None
        assert 0 <= n and (LOOPS - 1) * per_batch + n < total
        return n

    def count(self, per_batch, n):
        return self.b * per_batch + n


def wait(eng, at, sem, per_batch, n, times=1):
    value = at.b * (per_batch * times) + n * times
    if at.fixed and value <= 0:
        return
    assert at.fixed or n > 0
    eng.wait_ge(sem, value)


def wait_all(eng, at, waits, registers):
    values = [(sem, at.b * (per_batch * times) + n * times) for sem, per_batch, n, times in waits]
    if at.fixed:
        values = [(sem, value) for sem, value in values if value > 0]
    else:
        assert all(n > 0 for _, _, n, _ in waits)
        for (sem, value), register in zip(values, registers):
            eng.reg_mov(register, value)
        values = [(sem, register) for (sem, _), register in zip(values, registers)]
    for sem, value in values:
        eng.wait_ge(sem, value)


def all_steps(eng, step):
    for i in range(FIRST, LOOP_AT):
        step(At(0, i))
    with eng.Fori(0, LOOPS) as b:
        for i in range(LOOP_AT, LOOP_AT + SB):
            step(At(b, i))
    for i in range(LOOP_AT, LAST - LOOPS * SB):
        step(At(LOOPS, i))


def build(nc, x, ctx_in, masks, w_in, b_in, w_out, b_out, out):
    es = ExitStack()
    with es:
        def sb(name, shape, dt):
            return es.enter_context(nc.sbuf_tensor(name, shape, dt))

        def sem(name):
            return es.enter_context(nc.semaphore(name))

        es.enter_context(nc.allow_non_contiguous_dma(reason="bias vectors, once"))

        w_rows = sb("w_rows", [P, 3 * G, C], F32)
        wo_rows = sb("wo_rows", [P, G, C], F32)
        w_t = sb("w_t", [P, 4 * G * G, P], F32)
        w_hi = sb("w_hi", [P, 4 * G * G, P], F32R)
        w_lo = sb("w_lo", [P, 4 * G * G, P], F32R)
        b_in_col = sb("b_in_col", [P, 3 * G], F32)
        b_out_col = sb("b_out_col", [P, G], F32)
        q_bias = sb("q_bias", [P, G], F32)
        y_bias = sb("y_bias", [P, G], F32)
        ident = sb("ident", [P, P], F32)
        neg_w = sb("neg_w", [P, P], BF16)
        minus_half, minus_one, eps = (sb(name, [P, G], F32) for name in ("minus_half", "minus_one", "eps"))

        ctx_raw = [sb(f"ctx_raw{i}", [P, G, UNIT], F32) for i in range(2)]
        ctx_hi = [sb(f"ctx_hi{i}", [P, G, UNIT], F32R) for i in range(2)]
        ctx_lo = [sb(f"ctx_lo{i}", [P, G, UNIT], F32R) for i in range(2)]
        x_sb = [sb(f"x_sb{i}", [P, G, UNIT], F32) for i in range(2)]
        mask = [sb(f"mask{i}", [P, UNIT], F32) for i in range(4)]
        masked = [sb(f"masked{i}", [P, UNIT], BF16) for i in range(2)]
        q_sb = [sb(f"q_sb{i}", [P, 2, G, CU, 2 * CHUNK], F16) for i in range(2)]
        k_whole = [sb(f"k_whole{g}", [P, UNIT], F32) for g in range(G)]
        k_dense = [sb(f"k_dense{g}", [P, 2, UNIT], F16) for g in range(G)]
        k_sb = [sb(f"k_sb{i}", [P, G, 2, 2, UNIT], F16) for i in range(2)]
        v_sb = [sb(f"v_sb{i}", [P, 2, CU, 4 * 2 * CHUNK], F16) for i in range(2)]
        row_max = [sb(f"row_max{i}", [P, 8], F32) for i in range(2)]
        row_sum = [sb(f"row_sum{i}", [P, 8], F32) for i in range(2)]
        row_inv = [sb(f"row_inv{i}", [P, 8], F32) for i in range(4)]
        probs = [sb(f"probs{i}", [P, 4 * P], F32) for i in range(4)]
        pt_hi = [sb(f"pt_hi{i}", [P, 4 * P], F16) for i in range(2)]
        pt_lo = [sb(f"pt_lo{i}", [P, 4 * P], F16) for i in range(2)]
        o_hi = [sb(f"o_hi{i}", [P, G, UNIT], F32R) for i in range(2)]
        o_lo = [sb(f"o_lo{i}", [P, G, UNIT], F32R) for i in range(2)]
        o_whole = [sb(f"o_whole{i}", [P, G, UNIT // 2], F32) for i in range(2)]
        y_sb = [sb(f"y_sb{i}", [P, UNIT], F32) for i in range(2)]
        z_sb = sb("z_sb", [P, UB, G, UNIT], F32)
        stats = sb("stats", [P, G, UB, 6], F32)
        mean_var = sb("mean_var", [P, G, 2], F32)
        var_eps = sb("var_eps", [P, G], F32)
        rstd = sb("rstd", [P, G], F32)
        shift = sb("shift", [P, G], F32)
        out_sb = [sb(f"out_sb{i}", [P, UNIT], F32) for i in range(4)]

        def bank(name):
            return es.enter_context(nc.psum_tensor(name, [P, UNIT], F32))

        qk_bank = bank("qk_bank")
        vy_bank = bank("vy_bank")
        s_bank = [bank(f"s_bank{i}") for i in range(2)]
        t_bank = [bank(f"t_bank{i}") for i in range(2)]
        o_bank = [bank(f"o_bank{i}") for i in range(2)]

        w_loaded, consts_ready, w_turned, w_copied, w_split, w_hi_done = (
            sem("w_loaded"), sem("consts_ready"), sem("w_turned"), sem("w_copied"), sem("w_split"), sem("w_hi_done"))
        q_bias_ready, y_bias_psum, y_bias_ready = sem("q_bias_ready"), sem("y_bias_psum"), sem("y_bias_ready")
        ident_zeroed, neg_zeroed = sem("ident_zeroed"), sem("neg_zeroed")
        q_zeroed, k_zeroed, v_zeroed = sem("q_zeroed"), sem("k_zeroed"), sem("v_zeroed")
        ctx_loaded = [sem(f"ctx_loaded{i}") for i in range(2)]
        x_loaded = [sem(f"x_loaded{i}") for i in range(2)]
        mask_loaded = [sem(f"mask_loaded{i}") for i in range(4)]
        k_spread = [sem(f"k_spread{i}") for i in range(2)]
        out_free = [sem(f"out_free{i}") for i in range(4)]
        ctx_hi_done, ctx_lo_done, masked_done = sem("ctx_hi_done"), sem("ctx_lo_done"), sem("masked_done")
        qk_proj, qk_hi_done = sem("qk_proj"), sem("qk_hi_done")
        k_lo_done, q_lo_done = sem("k_lo_done"), sem("q_lo_done")
        v_proj, v_hi_done, v_lo_done = sem("v_proj"), sem("v_hi_done"), sem("v_lo_done")
        scored, max_done, shifted, exp_done = sem("scored"), sem("max_done"), sem("shifted"), sem("exp_done")
        sum_done, inv_done, normed = sem("sum_done"), sem("inv_done"), sem("normed")
        turned, pt_hi_done, pt_lo_done = sem("turned"), sem("pt_hi_done"), sem("pt_lo_done")
        attended, o_hi_done, o_lo_done = sem("attended"), sem("o_hi_done"), sem("o_lo_done")
        y_proj, y_masked, z_done = sem("y_proj"), sem("y_masked"), sem("z_done")
        aggregated, rstd_chain, rstd_done = sem("aggregated"), sem("rstd_chain"), sem("rstd_done")
        out_done = sem("out_done")

        def w_block(matrix, co, ci):
            return (matrix * G + co) * G + ci

        def scores_of(at, lag=0):
            return at.item(lag, 1, SB, STEPS)

        def qk_of(at, lag=0):
            return at.item(-5 + lag, 1, SB, UNITS * 4)

        def v_of(at, lag=0):
            return at.item(-2 + lag, 2, SB // 2, UNITS * 2)

        def o_of(at):
            return at.item(6, 2, SB // 2, UNITS * 2)

        def y_of(at, lag=0):
            return at.item(9 + lag, 2, SB // 2, UNITS * G)

        def ctx_load_of(at):
            return at.item(-12, 4, UB, UNITS)

        def ctx_split_of(at):
            return at.item(-6, 4, UB, UNITS)

        def mask_load_of(at):
            return at.item(-3, 4, UB, UNITS)

        def masked_of(at):
            return at.item(-1, 4, UB, UNITS)

        def x_load_of(at):
            return at.item(5, 4, UB, UNITS)

        def rstd_of(at):
            return at.item(25, SB, 1, N)

        def out_of(at, lag=0):
            for v in range(UB):
                n = at.item(26 + lag + v, SB, 1, N)
                if n is not None:
                    return n, v
            return None

        def o_tile(h):
            return o_bank[h % 2][:, :].rearrange("p (g t) -> p g t", g=G)

        def v_moves(v, half, part):
            moves = []
            psum = vy_bank[:, :].rearrange("p (a h s d) -> p a h s d", h=2 * G, s=2, d=DH)
            chunks = v_sb[v % 2][:, part, :, :].rearrange("p (a b) (h w) -> p a b h w", b=2, w=2 * CHUNK)
            for ab in range(2):
                for slot in range(2):
                    dst = chunks[64 * slot:64 * slot + 64, 2 * half:2 * half + 2, ab, :, DH * slot:DH * slot + DH]
                    moves.append((dst, psum[64 * ab:64 * ab + 64, :, :, slot, :]))
            return [(k == 3, m) for k, m in enumerate(moves)]

        block = es.enter_context(nc.Block())

        @block.sync
        def _(sp):
            sp.dma_start(w_rows[:, :, :], w_in.rearrange("(t p) c -> p t c", p=P)).then_inc(w_loaded, 16)
            sp.dma_start(wo_rows[:, :, :], w_out.rearrange("(t p) c -> p t c", p=P)).then_inc(w_loaded, 16)
            sp.dma_start(b_in_col[:, :], b_in.rearrange("(t p) -> p t", p=P)).then_inc(w_loaded, 16)
            sp.dma_start(b_out_col[:, :], b_out.rearrange("(t p) -> p t", p=P)).then_inc(w_loaded, 16)
            ctx_v = ctx_in.rearrange("n (g p) t -> n p g t", p=P)
            x_v = x.rearrange("n (g p) t -> n p g t", p=P)
            out_v = out.rearrange("n (g p) t -> n g p t", p=P)

            def tokens(v):
                t0 = v % UB * UNIT
                return slice(t0, t0 + UNIT)

            registers = [sp.alloc_register(f"wait{k}") for k in range(5)]

            def step(at):
                spread, waits = None, []
                j = qk_of(at, 1)
                if j is not None and j % 4 < G:
                    spread = v, g = j // 4, j % 4
                    if at.fixed and at.b == 0 and v < 2 and g == 0:
                        sp.wait_ge(k_zeroed, v + 1)
                    waits += [(k_lo_done, UB * G, v * G + g + 1, 1), (scored, SB, (v - 1) * SU, 1)]
                v_ctx, v_mask, v_x = ctx_load_of(at), mask_load_of(at), x_load_of(at)
                if v_ctx is not None:
                    waits.append((ctx_lo_done, UB * G, (v_ctx - 1) * G, 1))
                if v_mask is not None:
                    waits.append((y_masked, UB * G, (v_mask - 3) * G, 1))
                if v_x is not None:
                    waits.append((z_done, UB * G, (v_x - 1) * G, 1))
                wait_all(sp, at, waits, registers)
                if spread is not None:
                    v, g = spread
                    for quad in range(4):
                        rows = slice(DH * quad, DH * (quad + 1))
                        sp.dma_start(k_sb[v % 2][rows, g, :, quad % 2, :], k_dense[g][rows, :, :]) \
                          .then_inc(k_spread[v % 2], 16)
                if v_ctx is not None:
                    v = v_ctx
                    sp.dma_start(ctx_raw[v % 2][:, :, :], ctx_v[at.b + v // UB, :, :, tokens(v)]) \
                      .then_inc(ctx_loaded[v % 2], 16)
                if v_mask is not None:
                    v = v_mask
                    row = masks[at.b + v // UB, :, tokens(v)]
                    sp.dma_start(mask[v % 4][:, :], row.to_broadcast([P, UNIT])).then_inc(mask_loaded[v % 4], 16)
                if v_x is not None:
                    v = v_x
                    sp.dma_start(x_sb[v % 2][:, :, :], x_v[at.b + v // UB, :, :, tokens(v)]) \
                      .then_inc(x_loaded[v % 2], 16)
                bv = out_of(at, 1)
                if bv is not None:
                    n, v = bv
                    for g in range(G):
                        m = v * G + g
                        wait(sp, at, out_done, UB * G, n * UB * G + m + 1)
                        sp.dma_start(out_v[at.b + n, g, :, tokens(v)], out_sb[m % 4][:, :]) \
                          .then_inc(out_free[m % 4], 16)

            all_steps(sp, step)
            for s in out_free:
                sp.wait_ge(s, 16 * N * UB * G // 4 + 16)

        @block.gpsimd
        def _(pool):
            pool.memset(ident[:, :], 0.0).then_inc(ident_zeroed, 1)
            for tile, value in ((minus_half, -0.5), (minus_one, -1.0), (eps, EPS)):
                pool.memset(tile[:, :], value).then_inc(consts_ready, 1)
            pool.wait_ge(ident_zeroed, 1)
            pool.affine_select(out=ident[:, :], in_=ident[:, :], compare_op=ALU.not_equal, fill=1.0, base=0,
                               pattern=[[-1, P]], channel_multiplier=1).then_inc(consts_ready, 1)
            for i in range(2):
                pool.memset(k_sb[i][:, :, :, :, :].bitcast(F32), 0.0).then_inc(k_zeroed, 1)

            def step(at):
                j = qk_of(at, 1)
                if j is not None and j % 4 < G:
                    v, g = j // 4, j % 4
                    wait(pool, at, qk_hi_done, SB, j + 1)
                    pool.tensor_tensor(k_dense[g][:, LO, :], k_whole[g][:, :], k_dense[g][:, HI, :], ALU.subtract) \
                        .then_inc(k_lo_done, 1)
                r = scores_of(at, 2)
                if r is not None:
                    wait(pool, at, inv_done, SB, r + 1)
                    p3 = probs[r % 4][:, :].rearrange("p (a k) -> p a k", k=CHUNK)
                    inv = row_inv[r % 4][:, :].unsqueeze(2).to_broadcast([P, 8, CHUNK])
                    pool.tensor_tensor(p3, p3, inv, ALU.mult).then_inc(normed, 1)
                v = ctx_split_of(at)
                if v is not None:
                    wait(pool, at, ctx_hi_done, UB, v + 1)
                    for ci in range(G):
                        wait(pool, at, ctx_hi_done, UB, v + 1)
                        pool.tensor_tensor(ctx_lo[v % 2][:, ci, :], ctx_raw[v % 2][:, ci, :],
                                           ctx_hi[v % 2][:, ci, :].bitcast(F32), ALU.subtract).then_inc(ctx_lo_done, 1)
                n = rstd_of(at)
                if n is not None:
                    wait(pool, at, aggregated, 1, n + 1)
                    wait(pool, at, out_done, UB * G, n * UB * G)
                    pool.tensor_tensor(var_eps[:, :], mean_var[:, :, 1], eps[:, :], ALU.add).then_inc(rstd_chain, 1)
                    wait(pool, at, rstd_chain, 1, n + 1)
                    pool.tensor_tensor(rstd[:, :], var_eps[:, :], minus_half[:, :], ALU.pow).then_inc(rstd_done, 1)
                    wait(pool, at, rstd_done, 3, 3 * n + 1)
                    pool.tensor_tensor(shift[:, :], mean_var[:, :, 0], rstd[:, :], ALU.mult).then_inc(rstd_done, 1)
                    wait(pool, at, rstd_done, 3, 3 * n + 2)
                    pool.tensor_tensor(shift[:, :], shift[:, :], minus_one[:, :], ALU.mult).then_inc(rstd_done, 1)
                y = y_of(at, 1)
                if y is not None:
                    v, g = y // G, y % G
                    wait(pool, at, y_masked, UB * G, y + 1)
                    if g == 0:
                        wait(pool, at, x_loaded[v % 2], UB // 2, v // 2 + 1, 16)
                    wait(pool, at, out_done, UB * G, y - UB * G + 1)
                    pool.tensor_tensor(z_sb[:, v % UB, g, :], y_sb[y % 2][:, :], x_sb[v % 2][:, g, :], ALU.add) \
                        .then_inc(z_done, 1)
                h = o_of(at)
                if h is not None:
                    v, cols = h // 2, slice(256 * (h % 2), 256 * (h % 2) + 256)
                    wait(pool, at, o_hi_done, SB // 2, h + 1)
                    pool.tensor_tensor(o_lo[v % 2][:, :, cols], o_whole[h % 2][:, :, :],
                                       o_hi[v % 2][:, :, cols].bitcast(F32), ALU.subtract).then_inc(o_lo_done, 1)

            pool.wait_ge(k_zeroed, 2)
            all_steps(pool, step)

        @block.scalar
        def _(act):
            for s in out_free:
                act.sem_inc(s, 16)
            act.wait_ge(w_loaded, 64)
            nc.scalar.mul(q_bias[:, :], b_in_col[:, 0:G], SCALE).then_inc(q_bias_ready, 1)
            for m in range(4):
                act.wait_ge(w_turned, m + 1)
                src = (s_bank + t_bank)[m]
                nc.scalar.activation(w_t[:, 4 * m:4 * m + 4, :], src[:, :].rearrange("p (a c) -> p a c", c=P), ACT.Copy,
                                     scale=SCALE if m == 0 else 1.0).then_inc(w_copied, 1)
                act.wait_ge(w_copied, m + 1)
                nc.scalar.activation(w_hi[:, 4 * m:4 * m + 4, :], w_t[:, 4 * m:4 * m + 4, :], ACT.Copy) \
                    .then_inc(w_hi_done, 1)
            act.wait_ge(q_bias_ready, 1)

            def step(at):
                w = v_of(at, 1)
                if w is not None:
                    v, half = w // 2, w % 2
                    if at.fixed and at.b == 0 and v < 2 and half == 0:
                        act.wait_ge(v_zeroed, v + 1)
                    wait(act, at, v_proj, SB // 2, w + 1)
                    wait(act, at, attended, SB, 2 * (w - 4) + 2)
                    for last, (dst, src) in v_moves(v, half, HI):
                        ins = nc.scalar.activation(dst, src, ACT.Copy)
                        if last:
                            ins.then_inc(v_hi_done, 1)
                v = ctx_split_of(at)
                if v is not None:
                    wait(act, at, ctx_loaded[v % 2], UB // 2, v // 2 + 1, 16)
                    wait(act, at, v_proj, SB // 2, 2 * (v - 1))
                    nc.scalar.activation(ctx_hi[v % 2][:, :, :], ctx_raw[v % 2][:, :, :], ACT.Copy) \
                        .then_inc(ctx_hi_done, 1)
                h = o_of(at)
                if h is not None:
                    v, half = h // 2, h % 2
                    wait(act, at, attended, SB, 2 * h + 2)
                    wait(act, at, y_proj, UB * G, (v - 1) * G)
                    wait(act, at, o_lo_done, SB // 2, h - 1)
                    nc.scalar.activation(o_whole[h % 2][:, :, :], o_tile(h), ACT.Copy)
                    nc.scalar.activation(o_hi[v % 2][:, :, 256 * half:256 * half + 256], o_tile(h), ACT.Copy) \
                        .then_inc(o_hi_done, 1)
                r = scores_of(at, 1)
                if r is not None:
                    wait(act, at, shifted, SB, r + 1)
                    nc.scalar.activation(probs[r % 4][:, :], probs[r % 4][:, :], ACT.Exp).then_inc(exp_done, 1)
                bv = out_of(at)
                if bv is not None:
                    n, v = bv
                    wait(act, at, rstd_done, 3, 3 * n + 3)
                    for g in range(G):
                        m = v * G + g
                        wait(act, at, out_free[m % 4], 2, 2 * n + m // 4 + 1, 16)
                        nc.scalar.activation(out_sb[m % 4][:, :], z_sb[:, v, g, :], ACT.Identity,
                                             bias=shift[:, g:g + 1], scale=rstd[:, g:g + 1]).then_inc(out_done, 1)
                r = scores_of(at, 3)
                if r is not None:
                    wait(act, at, turned, SB, r + 1)
                    wait(act, at, attended, SB, r - 1)
                    nc.scalar.activation(pt_hi[r % 2][:, :], t_bank[r % 2][:, :], ACT.Copy).then_inc(pt_hi_done, 1)
                j = qk_of(at)
                if j is not None:
                    v, g = j // 4, j % 2
                    wait(act, at, qk_proj, SB, j + 1)
                    if j % 4 < G:
                        bias = b_in_col[:, G + g:G + g + 1]
                        wait(act, at, k_lo_done, UB * G, (v - 1) * G + g + 1)
                        nc.scalar.activation(k_whole[g][:, :], qk_bank[:, :], ACT.Identity, bias=bias)
                        wait(act, at, k_spread[(v - 1) % 2], UB // 2, (v + 1) // 2, 16 * 4 * G)
                        nc.scalar.activation(k_dense[g][:, HI, :], qk_bank[:, :], ACT.Identity, bias=bias) \
                            .then_inc(qk_hi_done, 1)
                    else:
                        if at.fixed and at.b == 0 and v < 2 and g == 0:
                            act.wait_ge(q_zeroed, v + 1)
                        wait(act, at, scored, SB, (v - 1) * SU)
                        for up in range(2):
                            rows, cols = slice(64 * up, 64 * up + 64), slice(CHUNK * up, CHUNK * up + CHUNK)
                            ins = nc.scalar.activation(
                                q_sb[v % 2][rows, HI, g, :, cols],
                                qk_bank[rows, :].rearrange("p (c t) -> p c t", t=CHUNK), ACT.Identity,
                                bias=q_bias[rows, g:g + 1])
                        ins.then_inc(qk_hi_done, 1)

            all_steps(act, step)

        @block.vector
        def _(dve):
            dve.memset(neg_w[:, :], 0.0).then_inc(neg_zeroed, 1)
            dve.wait_ge(neg_zeroed, 1)
            for r, part in enumerate(NEG_PARTS):
                dve.memset(neg_w[32 * r:32 * r + 1, :], part).then_inc(consts_ready, 1)
            for i in range(2):
                dve.memset(q_sb[i][:, :, :, :, :].bitcast(F32), 0.0).then_inc(q_zeroed, 1)
                dve.memset(v_sb[i][:, :, :, :].bitcast(F32), 0.0).then_inc(v_zeroed, 1)
            for m in range(4):
                dve.wait_ge(w_hi_done, m + 1)
                dve.tensor_tensor(w_lo[:, 4 * m:4 * m + 4, :], w_t[:, 4 * m:4 * m + 4, :],
                                  w_hi[:, 4 * m:4 * m + 4, :].bitcast(F32), ALU.subtract).then_inc(w_split, 1)
            dve.wait_ge(y_bias_psum, 1)
            dve.tensor_tensor(y_bias[:, :], o_bank[0][:, 0:G], b_out_col[:, :], ALU.add).then_inc(y_bias_ready, 1)
            dve.wait_ge(y_bias_ready, 1)

            def step(at):
                r = scores_of(at, 1)
                if r is not None:
                    s3 = s_bank[r % 2][:, :].rearrange("p (a k) -> p a k", k=CHUNK)
                    wait(dve, at, scored, SB, r + 1)
                    dve.tensor_reduce(row_max[r % 2][:, :], s3, AX.X, ALU.max).then_inc(max_done, 1)
                r = scores_of(at, 2)
                if r is not None:
                    p3 = probs[r % 4][:, :].rearrange("p (a k) -> p a k", k=CHUNK)
                    wait(dve, at, exp_done, SB, r + 1)
                    dve.tensor_reduce(row_sum[r % 2][:, :], p3, AX.X, ALU.add).then_inc(sum_done, 1)
                v = masked_of(at)
                if v is not None:
                    wait(dve, at, mask_loaded[v % 4], UB // 4, v // 4 + 1, 16)
                    wait(dve, at, scored, SB, (v - 1) * SU)
                    dve.tensor_scalar(masked[v % 2][:, :], mask[v % 4][:, :], 0.0, 0.0, ALU.is_gt, ALU.is_equal) \
                       .then_inc(masked_done, 1)
                y = y_of(at, 3)
                if y is not None:
                    v, g = y // G, y % G
                    last = y % (UB * G) == UB * G - 1
                    wait(dve, at, z_done, UB * G, y + 1)
                    if last:
                        wait(dve, at, rstd_done, 3, 3 * (y // (UB * G)))
                    dve.bn_stats(stats[:, g, v % UB, :], z_sb[:, v % UB, g, :])
                    if last:
                        dve.drain()
                        for g in range(G):
                            ins = dve.bn_aggr(mean_var[:, g, :], stats[:, g, :, :])
                        ins.then_inc(aggregated, 1)
                r = scores_of(at, 1)
                if r is not None:
                    s3 = s_bank[r % 2][:, :].rearrange("p (a k) -> p a k", k=CHUNK)
                    p3 = probs[r % 4][:, :].rearrange("p (a k) -> p a k", k=CHUNK)
                    wait(dve, at, max_done, SB, r + 1)
                    wait(dve, at, turned, SB, r - 3)
                    dve.tensor_tensor(p3, s3, row_max[r % 2][:, :].unsqueeze(2).to_broadcast([P, 8, CHUNK]),
                                      ALU.subtract).then_inc(shifted, 1)
                j = qk_of(at, 1)
                if j is not None and j % 4 >= G:
                    v, g = j // 4, j % 2
                    wait(dve, at, qk_hi_done, SB, j + 1)
                    for up in range(2):
                        rows, cols = slice(64 * up, 64 * up + 64), slice(CHUNK * up, CHUNK * up + CHUNK)
                        ins = dve.scalar_tensor_tensor(
                            out=q_sb[v % 2][rows, LO, g, :, cols],
                            in0=qk_bank[rows, :].rearrange("p (c t) -> p c t", t=CHUNK),
                            scalar=q_bias[rows, g:g + 1], in1=q_sb[v % 2][rows, HI, g, :, cols],
                            op0=ALU.add, op1=ALU.subtract)
                    ins.then_inc(q_lo_done, 1)
                r = scores_of(at, 2)
                if r is not None:
                    wait(dve, at, sum_done, SB, r + 1)
                    wait(dve, at, normed, SB, r - 3)
                    dve.reciprocal(row_inv[r % 4][:, :], row_sum[r % 2][:, :]).then_inc(inv_done, 1)
                r = scores_of(at, 4)
                if r is not None:
                    wait(dve, at, pt_hi_done, SB, r + 1)
                    dve.tensor_tensor(pt_lo[r % 2][:, :], t_bank[r % 2][:, :], pt_hi[r % 2][:, :], ALU.subtract) \
                       .then_inc(pt_lo_done, 1)
                w = v_of(at, 1)
                if w is not None:
                    v, half = w // 2, w % 2
                    wait(dve, at, v_hi_done, SB // 2, w + 1)
                    for (last, (dst, src)), (_, (hi, _)) in zip(v_moves(v, half, LO), v_moves(v, half, HI)):
                        ins = dve.tensor_tensor(dst, src, hi, ALU.subtract)
                        if last:
                            ins.then_inc(v_lo_done, 1)
                y = y_of(at, 1)
                if y is not None:
                    v, g = y // G, y % G
                    wait(dve, at, y_proj, UB * G, y + 1)
                    if g == 0:
                        wait(dve, at, mask_loaded[v % 4], UB // 4, v // 4 + 1, 16)
                    wait(dve, at, z_done, UB * G, y - 1)
                    dve.scalar_tensor_tensor(out=y_sb[y % 2][:, :], in0=vy_bank[:, :], scalar=y_bias[:, g:g + 1],
                                             in1=mask[v % 4][:, :], op0=ALU.add, op1=ALU.mult).then_inc(y_masked, 1)

            all_steps(dve, step)

        @block.tensor
        def _(pe):
            pe.wait_ge(w_loaded, 64)
            pe.wait_ge(consts_ready, 4 + len(NEG_PARTS))
            for m in range(4):
                rows = w_rows if m < 3 else wo_rows
                for co in range(G):
                    for ci in range(G):
                        k = co * G + ci
                        src = rows[:, m * G + co if m < 3 else co, ci * P:(ci + 1) * P]
                        ins = nc.tensor.transpose((s_bank + t_bank)[m][:, k * P:(k + 1) * P], src, ident[:, :])
                ins.then_inc(w_turned, 1)
            pe.wait_ge(w_copied, 4)
            for co in range(G):
                for ci in range(G):
                    ins = nc.tensor.matmul(o_bank[0][:, co:co + 1], w_t[:, w_block(3, co, ci), :],
                                           b_in_col[:, 2 * G + ci:2 * G + ci + 1], start=ci == 0, stop=ci == G - 1)
            ins.then_inc(y_bias_psum, 1)
            pe.wait_ge(w_split, 4)
            pe.wait_ge(y_bias_ready, 1)

            def project(dst, matrix, co, hi, lo):
                passes = [(w, a) for w, a in ((w_hi, hi), (w_lo, hi), (w_hi, lo))]
                for k, (w, a) in enumerate(passes):
                    for ci in range(G):
                        ins = nc.tensor.matmul(dst, w[:, w_block(matrix, co, ci), :], a[:, ci, :],
                                               start=k == 0 and ci == 0, stop=k == 2 and ci == G - 1)
                return ins

            def step(at):
                r = scores_of(at, 3)
                if r is not None:
                    wait(pe, at, normed, SB, r + 1)
                    wait(pe, at, pt_lo_done, SB, r - 1)
                    for k in range(4):
                        ins = nc.tensor.transpose(t_bank[r % 2][:, k * P:(k + 1) * P],
                                                  probs[r % 4][:, k * P:(k + 1) * P], ident[:, :])
                    ins.then_inc(turned, 1)
                r = scores_of(at)
                if r is not None:
                    v, q = r // SU, r % SU
                    if q == 0:
                        wait(pe, at, q_lo_done, UB * G, (v + 1) * G)
                        wait(pe, at, k_spread[v % 2], UB // 2, v // 2 + 1, 16 * 4 * G)
                        wait(pe, at, masked_done, UB, v + 1)
                    wait(pe, at, shifted, SB, r - 1)
                    cols = masked[v % 2][:, q * STEP:(q + 1) * STEP].rearrange("p (c t) -> p c t", t=CHUNK)
                    nc.tensor.matmul(
                        s_bank[r % 2][:, :].rearrange("p (c a t) -> p c a t", c=2, t=CHUNK), neg_w[:, :],
                        cols.unsqueeze(2).to_broadcast([P, 2, 4, CHUNK]),
                        start=True, stop=False, skip_group_check=True)
                    for c in range(2):
                        chunk = 2 * q + c
                        for g in range(G):
                            dst = s_bank[r % 2][:, (c * G + g) * P:(c * G + g + 1) * P]
                            for k, (a, b) in enumerate(((HI, HI), (HI, LO), (LO, HI))):
                                ins = nc.tensor.matmul(
                                    dst, q_sb[v % 2][:, a, g, chunk, :],
                                    k_sb[v % 2][:, g, b, :, chunk * CHUNK:(chunk + 1) * CHUNK],
                                    start=False, stop=k == 2, skip_group_check=True)
                    ins.then_inc(scored, 1)
                j = qk_of(at)
                if j is not None:
                    v = j // 4
                    if j % 4 == 0:
                        wait(pe, at, ctx_lo_done, UB * G, (v + 1) * G)
                    if 0 < j % 4 <= G:
                        wait(pe, at, qk_hi_done, SB, j)
                    else:
                        wait(pe, at, q_lo_done, UB * G, v * G + (j % 4 == 3))
                    project(qk_bank[:, :], 1 if j % 4 < G else 0, j % 2, ctx_hi[v % 2], ctx_lo[v % 2]) \
                        .then_inc(qk_proj, 1)
                w = v_of(at)
                if w is not None:
                    v, half = w // 2, w % 2
                    if at.fixed and at.count(SB // 2, w) <= 5:
                        wait(pe, at, v_lo_done, SB // 2, w)
                    else:
                        wait(pe, at, y_masked, UB * G, w - 5)
                    for a in range(2):
                        t0 = 256 * half + P * a
                        dst = vy_bank[:, C * a:C * a + C]
                        for k, (c, m) in enumerate(((ctx_hi, w_hi), (ctx_hi, w_lo), (ctx_lo, w_hi))):
                            for ci in range(G):
                                wv = m[:, w_block(2, 0, ci):w_block(2, 1, ci) + 1:G, :]
                                ins = nc.tensor.matmul(dst.rearrange("p (a c) -> p a c", a=G),
                                                       c[v % 2][:, ci, t0:t0 + P], wv,
                                                       start=k == 0 and ci == 0, stop=k == 2 and ci == G - 1)
                    ins.then_inc(v_proj, 1)
                r = scores_of(at, 4)
                if r is not None:
                    v, q = r // SU, r % SU
                    wait(pe, at, pt_lo_done, SB, r + 1)
                    if q % 2 == 0:
                        wait(pe, at, v_lo_done, SB // 2, 2 * v + q // 2 + 1)
                        wait(pe, at, o_hi_done, SB // 2, r // 2 - 1)
                    for c in range(2):
                        chunk = 2 * q + c
                        for g in range(G):
                            t0 = (q % 2) * STEP + c * CHUNK
                            dst = o_tile(r // 2)[:, g, t0:t0 + CHUNK]
                            k = 0
                            for low in range(2):
                                pcol = (c * G + g) * P + low * CHUNK
                                vcol = g * 4 * CHUNK + low * CHUNK
                                for part, pt in ((HI, pt_hi), (LO, pt_hi), (HI, pt_lo)):
                                    ins = nc.tensor.matmul(dst, v_sb[v % 2][:, part, chunk, vcol:vcol + P],
                                                           pt[r % 2][:, pcol:pcol + CHUNK],
                                                           start=k == 0, stop=k == 5)
                                    k += 1
                    ins.then_inc(attended, 1)
                y = y_of(at)
                if y is not None:
                    v, g = y // G, y % G
                    wait(pe, at, o_lo_done, SB // 2, 2 * v + 2)
                    if at.fixed:
                        pe.wait_ge(v_lo_done, min(at.count(SB // 2, y + 6), 2 * UNITS))
                        wait(pe, at, y_masked, UB * G, y)
                    else:
                        wait(pe, at, v_lo_done, SB // 2, y + 6)
                    project(vy_bank[:, :], 3, g, o_hi[v % 2], o_lo[v % 2]).then_inc(y_proj, 1)

            all_steps(pe, step)


_INS = ['x', 'ctx_4096', 'mask_Bx1x4096_ff1', 'L0_xattn_W_in', 'L0_xattn_b_in', 'L0_xattn_W_out', 'L0_xattn_b_out']
_OUTS = [((N, C, T), 'float32')]


def kernel(**inputs):
    import numpy as _np
    import concourse.bacc as _bacc
    from concourse import mybir as _mybir
    from concourse.bass_utils import run_bass_kernel_spmd as _run

    nc = _bacc.Bacc("TRN2", target_bir_lowering=False, num_devices=1)
    arrays, args = {}, []
    for name in _INS:
        a = _np.ascontiguousarray(inputs[name])
        arrays[f"in_{name}_dram"] = a
        args.append(nc.dram_tensor(f"in_{name}_dram", a.shape, _mybir.dt.from_np(a.dtype), kind="ExternalInput").ap())
    for i, (shape, dtype) in enumerate(_OUTS):
        dt = _mybir.dt.from_np(_np.dtype(dtype))
        args.append(nc.dram_tensor(f"out_{i}_dram", shape, dt, kind="ExternalOutput").ap())
    build(nc, *args)
    r = _run(nc, [arrays], core_ids=[0])
    got = tuple(r.results[0][f"out_{i}_dram"] for i in range(len(_OUTS)))
    return got[0]
```

```python
from contextlib import ExitStack

import concourse.bass as bass
from concourse import mybir

F32 = mybir.dt.float32
F32R = mybir.dt.float32r
F16 = mybir.dt.float16
BF16 = mybir.dt.bfloat16
ALU = mybir.AluOpType
ACT = mybir.ActivationFunctionType
AX = mybir.AxisListType

P = 128
N, C, T = 16, 256, 2048
HEADS, CHUNK = 8, 64
DH = C // HEADS
G = C // P
UNIT = 512
STEP = 128
UB = T // UNIT
SB = T // STEP
SU = UNIT // STEP
CU = UNIT // CHUNK
UNITS, STEPS = N * UB, N * SB
HI, LO = 0, 1
EPS = 1e-5
NEG = -1e9
SCALE = 1.0 / DH ** 0.5
NEG_PARTS = (-998244352.0, -1753088.0, -2560.0)

W_Q, W_K, W_V, W_OUT = range(4)
W_ORDER = (W_K, W_Q, W_V, W_OUT)

FIRST = -12
LOOP_AT = 27
LOOPS = N - 3
LAST = STEPS + 15


class At:

    def __init__(self, b, i):
        self.b, self.i = b, i
        self.fixed = isinstance(b, int)

    def item(self, lag, period, per_batch, total):
        i = self.i - lag
        if i % period:
            return None
        n = i // period
        if self.fixed:
            return n if 0 <= self.b * per_batch + n < total else None
        assert 0 <= n and (LOOPS - 1) * per_batch + n < total
        return n

    def count(self, per_batch, n):
        return self.b * per_batch + n


def wait(eng, at, sem, per_batch, n, times=1):
    value = at.b * (per_batch * times) + n * times
    if at.fixed and value <= 0:
        return
    assert at.fixed or n > 0
    eng.wait_ge(sem, value)


def wait_all(eng, at, waits, registers):
    values = [(sem, at.b * (per_batch * times) + n * times) for sem, per_batch, n, times in waits]
    if at.fixed:
        values = [(sem, value) for sem, value in values if value > 0]
    else:
        assert all(n > 0 for _, _, n, _ in waits)
        for (sem, value), register in zip(values, registers):
            eng.reg_mov(register, value)
        values = [(sem, register) for (sem, _), register in zip(values, registers)]
    for sem, value in values:
        eng.wait_ge(sem, value)


def all_steps(eng, step):
    for i in range(FIRST, LOOP_AT):
        step(At(0, i))
    with eng.Fori(0, LOOPS) as b:
        for i in range(LOOP_AT, LOOP_AT + SB):
            step(At(b, i))
    for i in range(LOOP_AT, LAST - LOOPS * SB):
        step(At(LOOPS, i))


def build(nc, x, ctx_in, masks, w_in, b_in, w_out, b_out, out):
    es = ExitStack()
    with es:
        def sb(name, shape, dt):
            return es.enter_context(nc.sbuf_tensor(name, shape, dt))

        def sem(name):
            return es.enter_context(nc.semaphore(name))

        es.enter_context(nc.allow_non_contiguous_dma(reason="bias vectors, once"))

        w_rows = sb("w_rows", [P, 4 * G, C], F32)
        w_t = sb("w_t", [P, 4 * G * G, P], F32)
        w_hi = sb("w_hi", [P, 4 * G * G, P], F32R)
        w_lo = sb("w_lo", [P, 4 * G * G, P], F32R)
        b_in_col = sb("b_in_col", [P, 3 * G], F32)
        b_out_col = sb("b_out_col", [P, G], F32)
        q_bias = sb("q_bias", [P, G], F32)
        y_bias = sb("y_bias", [P, G], F32)
        ident = sb("ident", [P, P], F32)
        neg_w = sb("neg_w", [P, P], BF16)
        minus_half, minus_one, eps = (sb(name, [P, G], F32) for name in ("minus_half", "minus_one", "eps"))

        ctx_raw = [sb(f"ctx_raw{i}", [P, G, UNIT], F32) for i in range(2)]
        ctx_hi = [sb(f"ctx_hi{i}", [P, G, UNIT], F32R) for i in range(2)]
        ctx_lo = [sb(f"ctx_lo{i}", [P, G, UNIT], F32R) for i in range(2)]
        x_sb = [sb(f"x_sb{i}", [P, G, UNIT], F32) for i in range(2)]
        mask = [sb(f"mask{i}", [P, UNIT], F32) for i in range(4)]
        masked = [sb(f"masked{i}", [P, UNIT], BF16) for i in range(2)]
        q_sb = [sb(f"q_sb{i}", [P, 2, G, CU, 2 * CHUNK], F16) for i in range(2)]
        k_whole = [sb(f"k_whole{g}", [P, UNIT], F32) for g in range(G)]
        k_dense = [sb(f"k_dense{g}", [P, 2, UNIT], F16) for g in range(G)]
        k_sb = [sb(f"k_sb{i}", [P, G, 2, 2, UNIT], F16) for i in range(2)]
        v_sb = [sb(f"v_sb{i}", [P, 2, CU, 4 * 2 * CHUNK], F16) for i in range(2)]
        row_max = [sb(f"row_max{i}", [P, 8], F32) for i in range(2)]
        row_sum = [sb(f"row_sum{i}", [P, 8], F32) for i in range(2)]
        row_inv = [sb(f"row_inv{i}", [P, 8], F32) for i in range(4)]
        probs = [sb(f"probs{i}", [P, 4 * P], F32) for i in range(4)]
        pt_hi = [sb(f"pt_hi{i}", [P, 4 * P], F16) for i in range(2)]
        pt_whole = w_t[:, 0:4, :].rearrange("p a c -> p (a c)")
        pt_lo = [sb(f"pt_lo{i}", [P, 4 * P], F16) for i in range(2)]
        o_hi = [sb(f"o_hi{i}", [P, G, UNIT], F32R) for i in range(2)]
        o_lo = [sb(f"o_lo{i}", [P, G, UNIT], F32R) for i in range(2)]
        o_whole = [sb(f"o_whole{i}", [P, G, UNIT // 2], F32) for i in range(2)]
        y_sb = [sb(f"y_sb{i}", [P, UNIT], F32) for i in range(2)]
        z_sb = sb("z_sb", [P, UB, G, UNIT], F32)
        stats = sb("stats", [P, G, UB, 6], F32)
        mean_var = sb("mean_var", [P, G, 2], F32)
        var_eps = sb("var_eps", [P, G], F32)
        rstd = sb("rstd", [P, G], F32)
        shift = sb("shift", [P, G], F32)
        out_tiles = [sb(f"out_sb{i}", [P, UNIT], F32)[:, :] for i in range(UB * G // 2)]
        out_tiles += [w_rows[:, 2 * i:2 * i + 2, :].rearrange("p a c -> p (a c)") for i in range(UB * G // 2)]

        def bank(name):
            return es.enter_context(nc.psum_tensor(name, [P, UNIT], F32))

        qk_bank = bank("qk_bank")
        vy_bank = bank("vy_bank")
        s_bank = [bank(f"s_bank{i}") for i in range(2)]
        t_bank = [bank(f"t_bank{i}") for i in range(2)]
        o_bank = [bank(f"o_bank{i}") for i in range(2)]

        w_loaded = [sem(f"w_loaded{k}") for k in range(4)]
        b_loaded, consts_ready, w_turned, w_copied, w_split, w_hi_done = (
            sem("b_loaded"), sem("consts_ready"), sem("w_turned"), sem("w_copied"), sem("w_split"), sem("w_hi_done"))
        q_bias_ready, y_bias_psum, y_bias_ready = sem("q_bias_ready"), sem("y_bias_psum"), sem("y_bias_ready")
        ident_zeroed, neg_zeroed = sem("ident_zeroed"), sem("neg_zeroed")
        q_zeroed, k_zeroed, v_zeroed = sem("q_zeroed"), sem("k_zeroed"), sem("v_zeroed")
        ctx_loaded = [sem(f"ctx_loaded{i}") for i in range(2)]
        x_loaded = [sem(f"x_loaded{i}") for i in range(2)]
        mask_loaded = [sem(f"mask_loaded{i}") for i in range(4)]
        k_spread = [sem(f"k_spread{i}") for i in range(2)]
        stored = [sem(f"stored{i}") for i in range(UB * G)]
        ctx_hi_done, ctx_lo_done, masked_done = sem("ctx_hi_done"), sem("ctx_lo_done"), sem("masked_done")
        qk_proj, qk_hi_done = sem("qk_proj"), sem("qk_hi_done")
        k_lo_done, q_lo_done = sem("k_lo_done"), sem("q_lo_done")
        v_proj, v_hi_done, v_lo_done = sem("v_proj"), sem("v_hi_done"), sem("v_lo_done")
        scored, max_done, shifted, exp_done = sem("scored"), sem("max_done"), sem("shifted"), sem("exp_done")
        sum_done, inv_done, normed = sem("sum_done"), sem("inv_done"), sem("normed")
        turned, pt_hi_done = sem("turned"), sem("pt_hi_done")
        pt_lo_done, pt_lo_last_done = sem("pt_lo_done"), sem("pt_lo_last_done")
        attended, o_hi_done, o_lo_done = sem("attended"), sem("o_hi_done"), sem("o_lo_done")
        y_proj, y_masked, z_done = sem("y_proj"), sem("y_masked"), sem("z_done")
        aggregated, rstd_chain, rstd_done = sem("aggregated"), sem("rstd_chain"), sem("rstd_done")
        out_done = sem("out_done")

        def w_block(matrix, co, ci):
            return (matrix * G + co) * G + ci

        def scores_of(at, lag=0):
            return at.item(lag, 1, SB, STEPS)

        def is_last(r):
            return r % SU == SU - 1

        def wait_pt_lo(eng, at, r):
            if is_last(r):
                wait(eng, at, pt_lo_last_done, UB, r // SU + 1)
            else:
                wait(eng, at, pt_lo_done, UB * (SU - 1), r // SU * (SU - 1) + r % SU + 1)

        def qk_of(at, lag=0):
            return at.item(-5 + lag, 1, SB, UNITS * 4)

        def v_of(at, lag=0):
            return at.item(-2 + lag, 2, SB // 2, UNITS * 2)

        def o_of(at):
            return at.item(6, 2, SB // 2, UNITS * 2)

        def y_of(at, lag=0):
            return at.item(9 + lag, 2, SB // 2, UNITS * G)

        def first_unit(at, v):
            return at.fixed and at.b == 0 and v == 0

        def ctx_load_of(at):
            return at.item(-12, 4, UB, UNITS)

        def ctx_split_of(at, lag=0):
            return at.item(-7 + lag, 4, UB, UNITS)

        def mask_load_of(at):
            return at.item(-3, 4, UB, UNITS)

        def masked_of(at):
            return at.item(-1, 4, UB, UNITS)

        def x_load_of(at):
            return at.item(5, 4, UB, UNITS)

        def rstd_of(at):
            return at.item(25, SB, 1, N)

        def out_of(at, lag=0):
            for v in range(UB):
                n = at.item(26 + lag + v, SB, 1, N)
                if n is not None:
                    return n, v
            return None

        def o_tile(h):
            return o_bank[h % 2][:, :].rearrange("p (g t) -> p g t", g=G)

        def v_moves(v, half, part):
            moves = []
            psum = vy_bank[:, :].rearrange("p (a h s d) -> p a h s d", h=2 * G, s=2, d=DH)
            chunks = v_sb[v % 2][:, part, :, :].rearrange("p (a b) (h w) -> p a b h w", b=2, w=2 * CHUNK)
            for ab in range(2):
                for slot in range(2):
                    dst = chunks[64 * slot:64 * slot + 64, 2 * half:2 * half + 2, ab, :, DH * slot:DH * slot + DH]
                    moves.append((dst, psum[64 * ab:64 * ab + 64, :, :, slot, :]))
            return [(k == 3, m) for k, m in enumerate(moves)]

        block = es.enter_context(nc.Block())

        @block.sync
        def _(sp):
            ctx_v = ctx_in.rearrange("n (g p) t -> n p g t", p=P)
            x_v = x.rearrange("n (g p) t -> n p g t", p=P)
            out_v = out.rearrange("n (g p) t -> n g p t", p=P)

            def tokens(v):
                t0 = v % UB * UNIT
                return slice(t0, t0 + UNIT)

            def load_context(at):
                v = ctx_load_of(at)
                sp.dma_start(ctx_raw[v % 2][:, :, :], ctx_v[at.b + v // UB, :, :, tokens(v)]) \
                  .then_inc(ctx_loaded[v % 2], 16)

            for k, m in enumerate(W_ORDER):
                if m == W_OUT:
                    src = w_out.rearrange("(t p) c -> p t c", p=P)
                else:
                    src = w_in.rearrange("(m t p) c -> m p t c", p=P, t=G)[m, :, :, :]
                sp.dma_start(w_rows[:, m * G:(m + 1) * G, :], src).then_inc(w_loaded[k], 16)
                if k == 0:
                    load_context(At(0, FIRST))
            sp.dma_start(b_in_col[:, :], b_in.rearrange("(t p) -> p t", p=P)).then_inc(b_loaded, 16)
            sp.dma_start(b_out_col[:, :], b_out.rearrange("(t p) -> p t", p=P)).then_inc(b_loaded, 16)
            registers = [sp.alloc_register(f"wait{k}") for k in range(5)]

            def step(at):
                spread, waits = None, []
                j = qk_of(at, 1)
                if j is not None and j % 4 < G:
                    spread = v, g = j // 4, j % 4
                    if at.fixed and at.b == 0 and v < 2 and g == 0:
                        sp.wait_ge(k_zeroed, v + 1)
                    waits += [(k_lo_done, UB * G, v * G + g + 1, 1), (scored, SB, (v - 1) * SU, 1)]
                v_ctx, v_mask, v_x = ctx_load_of(at), mask_load_of(at), x_load_of(at)
                if v_ctx is not None:
                    waits.append((ctx_lo_done, UB * G, (v_ctx - 1) * G, 1))
                if v_mask is not None:
                    waits.append((y_masked, UB * G, (v_mask - 3) * G, 1))
                if v_x is not None:
                    waits.append((z_done, UB * G, (v_x - 1) * G, 1))
                wait_all(sp, at, waits, registers)
                if spread is not None:
                    v, g = spread
                    for quad in range(4):
                        rows = slice(DH * quad, DH * (quad + 1))
                        sp.dma_start(k_sb[v % 2][rows, g, :, quad % 2, :], k_dense[g][rows, :, :]) \
                          .then_inc(k_spread[v % 2], 16)
                if v_ctx is not None and not first_unit(at, v_ctx):
                    load_context(at)
                if v_mask is not None:
                    v = v_mask
                    row = masks[at.b + v // UB, :, tokens(v)]
                    sp.dma_start(mask[v % 4][:, :], row.to_broadcast([P, UNIT])).then_inc(mask_loaded[v % 4], 16)
                if v_x is not None:
                    v = v_x
                    sp.dma_start(x_sb[v % 2][:, :, :], x_v[at.b + v // UB, :, :, tokens(v)]) \
                      .then_inc(x_loaded[v % 2], 16)
                bv = out_of(at, 1)
                if bv is not None:
                    n, v = bv
                    for g in range(G):
                        m = v * G + g
                        wait(sp, at, out_done, UB * G, n * UB * G + m + 1)
                        sp.dma_start(out_v[at.b + n, g, :, tokens(v)], out_tiles[m]).then_inc(stored[m], 16)

            all_steps(sp, step)
            for s in stored:
                sp.wait_ge(s, 16 * N + 16)

        @block.gpsimd
        def _(pool):
            pool.memset(ident[:, :], 0.0).then_inc(ident_zeroed, 1)
            for tile, value in ((minus_half, -0.5), (minus_one, -1.0), (eps, EPS)):
                pool.memset(tile[:, :], value).then_inc(consts_ready, 1)
            pool.wait_ge(ident_zeroed, 1)
            pool.affine_select(out=ident[:, :], in_=ident[:, :], compare_op=ALU.not_equal, fill=1.0, base=0,
                               pattern=[[-1, P]], channel_multiplier=1).then_inc(consts_ready, 1)
            for i in range(2):
                pool.memset(k_sb[i][:, :, :, :, :].bitcast(F32), 0.0).then_inc(k_zeroed, 1)

            def step(at):
                j = qk_of(at, 1)
                if j is not None and j % 4 < G:
                    v, g = j // 4, j % 4
                    wait(pool, at, qk_hi_done, SB, j + 1)
                    pool.tensor_tensor(k_dense[g][:, LO, :], k_whole[g][:, :], k_dense[g][:, HI, :], ALU.subtract) \
                        .then_inc(k_lo_done, 1)
                r = scores_of(at, 2)
                if r is not None:
                    wait(pool, at, inv_done, SB, r + 1)
                    p3 = probs[r % 4][:, :].rearrange("p (a k) -> p a k", k=CHUNK)
                    inv = row_inv[r % 4][:, :].unsqueeze(2).to_broadcast([P, 8, CHUNK])
                    pool.tensor_tensor(p3, p3, inv, ALU.mult).then_inc(normed, 1)
                n = rstd_of(at)
                if n is not None:
                    wait(pool, at, aggregated, 1, n + 1)
                    wait(pool, at, out_done, UB * G, n * UB * G)
                    pool.tensor_tensor(var_eps[:, :], mean_var[:, :, 1], eps[:, :], ALU.add).then_inc(rstd_chain, 1)
                    wait(pool, at, rstd_chain, 1, n + 1)
                    pool.tensor_tensor(rstd[:, :], var_eps[:, :], minus_half[:, :], ALU.pow).then_inc(rstd_done, 1)
                    wait(pool, at, rstd_done, 3, 3 * n + 1)
                    pool.tensor_tensor(shift[:, :], mean_var[:, :, 0], rstd[:, :], ALU.mult).then_inc(rstd_done, 1)
                    wait(pool, at, rstd_done, 3, 3 * n + 2)
                    pool.tensor_tensor(shift[:, :], shift[:, :], minus_one[:, :], ALU.mult).then_inc(rstd_done, 1)
                r = scores_of(at, 3)
                if r is not None and is_last(r):
                    wait(pool, at, pt_hi_done, SB, r + 1)
                    pool.tensor_tensor(pt_lo[r % 2][:, :], pt_whole, pt_hi[r % 2][:, :], ALU.subtract) \
                        .then_inc(pt_lo_last_done, 1)
                h = o_of(at)
                if h is not None:
                    v, cols = h // 2, slice(256 * (h % 2), 256 * (h % 2) + 256)
                    wait(pool, at, o_hi_done, SB // 2, h + 1)
                    pool.tensor_tensor(o_lo[v % 2][:, :, cols], o_whole[h % 2][:, :, :],
                                       o_hi[v % 2][:, :, cols].bitcast(F32), ALU.subtract).then_inc(o_lo_done, 1)
                v = ctx_split_of(at)
                if v is not None:
                    wait(pool, at, ctx_hi_done, UB, v + 1)
                    for ci in range(G):
                        wait(pool, at, ctx_hi_done, UB, v + 1)
                        pool.tensor_tensor(ctx_lo[v % 2][:, ci, :], ctx_raw[v % 2][:, ci, :],
                                           ctx_hi[v % 2][:, ci, :].bitcast(F32), ALU.subtract).then_inc(ctx_lo_done, 1)
                y = y_of(at)
                if y is not None:
                    v, g = y // G, y % G
                    wait(pool, at, y_masked, UB * G, y + 1)
                    if g == 0:
                        wait(pool, at, x_loaded[v % 2], UB // 2, v // 2 + 1, 16)
                    wait(pool, at, out_done, UB * G, y - UB * G + 1)
                    pool.tensor_tensor(z_sb[:, v % UB, g, :], y_sb[y % 2][:, :], x_sb[v % 2][:, g, :], ALU.add) \
                        .then_inc(z_done, 1)

            pool.wait_ge(k_zeroed, 2)
            all_steps(pool, step)

        @block.scalar
        def _(act):
            for s in stored:
                act.sem_inc(s, 16)

            def split_context(at):
                v = ctx_split_of(at)
                wait(act, at, ctx_loaded[v % 2], UB // 2, v // 2 + 1, 16)
                wait(act, at, v_proj, SB // 2, 2 * (v - 1))
                nc.scalar.activation(ctx_hi[v % 2][:, :, :], ctx_raw[v % 2][:, :, :], ACT.Copy) \
                    .then_inc(ctx_hi_done, 1)

            for k, m in enumerate(W_ORDER):
                act.wait_ge(w_turned, k + 1)
                src = (s_bank + t_bank)[k][:, :].rearrange("p (a c) -> p a c", c=P)
                scale = SCALE if m == W_Q else 1.0
                nc.scalar.activation(w_hi[:, 4 * m:4 * m + 4, :], src, ACT.Copy, scale=scale).then_inc(w_hi_done, 1)
                nc.scalar.activation(w_t[:, 4 * m:4 * m + 4, :], src, ACT.Copy, scale=scale).then_inc(w_copied, 1)
                if k == 1:
                    split_context(At(0, -7))
            act.wait_ge(b_loaded, 32)
            nc.scalar.mul(q_bias[:, :], b_in_col[:, 0:G], SCALE).then_inc(q_bias_ready, 1)
            act.wait_ge(q_bias_ready, 1)

            def step(at):
                w = v_of(at, 1)
                if w is not None:
                    v, half = w // 2, w % 2
                    if at.fixed and at.b == 0 and v < 2 and half == 0:
                        act.wait_ge(v_zeroed, v + 1)
                    wait(act, at, v_proj, SB // 2, w + 1)
                    wait(act, at, attended, SB, 2 * (w - 4) + 2)
                    for last, (dst, src) in v_moves(v, half, HI):
                        ins = nc.scalar.activation(dst, src, ACT.Copy)
                        if last:
                            ins.then_inc(v_hi_done, 1)
                bv = out_of(at)
                if bv is not None:
                    n, v = bv
                    wait(act, at, rstd_done, 3, 3 * n + 3)
                    for g in range(G):
                        m = v * G + g
                        wait(act, at, stored[m], 1, n + 1, 16)
                        nc.scalar.activation(out_tiles[m], z_sb[:, v, g, :], ACT.Identity,
                                             bias=shift[:, g:g + 1], scale=rstd[:, g:g + 1]).then_inc(out_done, 1)
                h = o_of(at)
                if h is not None:
                    v, half = h // 2, h % 2
                    wait(act, at, attended, SB, 2 * h + 2)
                    wait(act, at, y_proj, UB * G, (v - 1) * G)
                    wait(act, at, o_lo_done, SB // 2, h - 1)
                    nc.scalar.activation(o_whole[h % 2][:, :, :], o_tile(h), ACT.Copy)
                    nc.scalar.activation(o_hi[v % 2][:, :, 256 * half:256 * half + 256], o_tile(h), ACT.Copy) \
                        .then_inc(o_hi_done, 1)
                r = scores_of(at, 1)
                if r is not None:
                    wait(act, at, shifted, SB, r + 1)
                    nc.scalar.activation(probs[r % 4][:, :], probs[r % 4][:, :], ACT.Exp).then_inc(exp_done, 1)
                j = qk_of(at)
                if j is not None:
                    v, g = j // 4, j % 2
                    wait(act, at, qk_proj, SB, j + 1)
                    if j % 4 < G:
                        bias = b_in_col[:, G + g:G + g + 1]
                        wait(act, at, k_lo_done, UB * G, (v - 1) * G + g + 1)
                        nc.scalar.activation(k_whole[g][:, :], qk_bank[:, :], ACT.Identity, bias=bias)
                        wait(act, at, k_spread[(v - 1) % 2], UB // 2, (v + 1) // 2, 16 * 4 * G)
                        nc.scalar.activation(k_dense[g][:, HI, :], qk_bank[:, :], ACT.Identity, bias=bias) \
                            .then_inc(qk_hi_done, 1)
                    else:
                        if at.fixed and at.b == 0 and v < 2 and g == 0:
                            act.wait_ge(q_zeroed, v + 1)
                        wait(act, at, scored, SB, (v - 1) * SU)
                        for up in range(2):
                            rows, cols = slice(64 * up, 64 * up + 64), slice(CHUNK * up, CHUNK * up + CHUNK)
                            ins = nc.scalar.activation(
                                q_sb[v % 2][rows, HI, g, :, cols],
                                qk_bank[rows, :].rearrange("p (c t) -> p c t", t=CHUNK), ACT.Identity,
                                bias=q_bias[rows, g:g + 1])
                        ins.then_inc(qk_hi_done, 1)
                v = ctx_split_of(at)
                if v is not None and not first_unit(at, v):
                    split_context(at)
                r = scores_of(at, 3)
                if r is not None:
                    wait(act, at, turned, SB, r + 1)
                    wait(act, at, attended, SB, r - 1)
                    if is_last(r):
                        wait(act, at, pt_lo_last_done, UB, r // SU)
                        nc.scalar.activation(pt_whole, t_bank[r % 2][:, :], ACT.Copy)
                    nc.scalar.activation(pt_hi[r % 2][:, :], t_bank[r % 2][:, :], ACT.Copy).then_inc(pt_hi_done, 1)

            all_steps(act, step)

        @block.vector
        def _(dve):
            dve.memset(neg_w[:, :], 0.0).then_inc(neg_zeroed, 1)
            dve.wait_ge(neg_zeroed, 1)
            for r, part in enumerate(NEG_PARTS):
                dve.memset(neg_w[32 * r:32 * r + 1, :], part).then_inc(consts_ready, 1)

            def zero(i):
                dve.memset(q_sb[i][:, :, :, :, :].bitcast(F32), 0.0).then_inc(q_zeroed, 1)
                dve.memset(v_sb[i][:, :, :, :].bitcast(F32), 0.0).then_inc(v_zeroed, 1)

            zero(0)
            for k, m in enumerate(W_ORDER):
                dve.wait_ge(w_copied, k + 1)
                dve.tensor_tensor(w_lo[:, 4 * m:4 * m + 4, :], w_t[:, 4 * m:4 * m + 4, :],
                                  w_hi[:, 4 * m:4 * m + 4, :].bitcast(F32), ALU.subtract).then_inc(w_split, 1)
            dve.wait_ge(y_bias_psum, 1)
            dve.tensor_tensor(y_bias[:, :], o_bank[0][:, 0:G], b_out_col[:, :], ALU.add).then_inc(y_bias_ready, 1)
            dve.wait_ge(y_bias_ready, 1)
            zero(1)

            def step(at):
                r = scores_of(at, 1)
                if r is not None:
                    s3 = s_bank[r % 2][:, :].rearrange("p (a k) -> p a k", k=CHUNK)
                    wait(dve, at, scored, SB, r + 1)
                    dve.tensor_reduce(row_max[r % 2][:, :], s3, AX.X, ALU.max).then_inc(max_done, 1)
                r = scores_of(at, 2)
                if r is not None:
                    p3 = probs[r % 4][:, :].rearrange("p (a k) -> p a k", k=CHUNK)
                    wait(dve, at, exp_done, SB, r + 1)
                    dve.tensor_reduce(row_sum[r % 2][:, :], p3, AX.X, ALU.add).then_inc(sum_done, 1)
                j = qk_of(at, 1)
                if j is not None and j % 4 >= G:
                    v, g = j // 4, j % 2
                    wait(dve, at, qk_hi_done, SB, j + 1)
                    for up in range(2):
                        rows, cols = slice(64 * up, 64 * up + 64), slice(CHUNK * up, CHUNK * up + CHUNK)
                        ins = dve.scalar_tensor_tensor(
                            out=q_sb[v % 2][rows, LO, g, :, cols],
                            in0=qk_bank[rows, :].rearrange("p (c t) -> p c t", t=CHUNK),
                            scalar=q_bias[rows, g:g + 1], in1=q_sb[v % 2][rows, HI, g, :, cols],
                            op0=ALU.add, op1=ALU.subtract)
                    ins.then_inc(q_lo_done, 1)
                y = y_of(at, 1)
                if y is not None:
                    v, g = y // G, y % G
                    wait(dve, at, y_proj, UB * G, y + 1)
                    if g == 0:
                        wait(dve, at, mask_loaded[v % 4], UB // 4, v // 4 + 1, 16)
                    wait(dve, at, z_done, UB * G, y - 1)
                    dve.scalar_tensor_tensor(out=y_sb[y % 2][:, :], in0=vy_bank[:, :], scalar=y_bias[:, g:g + 1],
                                             in1=mask[v % 4][:, :], op0=ALU.add, op1=ALU.mult).then_inc(y_masked, 1)
                r = scores_of(at, 1)
                if r is not None:
                    s3 = s_bank[r % 2][:, :].rearrange("p (a k) -> p a k", k=CHUNK)
                    p3 = probs[r % 4][:, :].rearrange("p (a k) -> p a k", k=CHUNK)
                    wait(dve, at, max_done, SB, r + 1)
                    wait(dve, at, turned, SB, r - 3)
                    dve.tensor_tensor(p3, s3, row_max[r % 2][:, :].unsqueeze(2).to_broadcast([P, 8, CHUNK]),
                                      ALU.subtract).then_inc(shifted, 1)
                r = scores_of(at, 4)
                if r is not None and not is_last(r):
                    wait(dve, at, pt_hi_done, SB, r + 1)
                    dve.tensor_tensor(pt_lo[r % 2][:, :], t_bank[r % 2][:, :], pt_hi[r % 2][:, :], ALU.subtract) \
                       .then_inc(pt_lo_done, 1)
                r = scores_of(at, 2)
                if r is not None:
                    wait(dve, at, sum_done, SB, r + 1)
                    wait(dve, at, normed, SB, r - 3)
                    dve.reciprocal(row_inv[r % 4][:, :], row_sum[r % 2][:, :]).then_inc(inv_done, 1)
                w = v_of(at, 1)
                if w is not None:
                    v, half = w // 2, w % 2
                    wait(dve, at, v_hi_done, SB // 2, w + 1)
                    for (last, (dst, src)), (_, (hi, _)) in zip(v_moves(v, half, LO), v_moves(v, half, HI)):
                        ins = dve.tensor_tensor(dst, src, hi, ALU.subtract)
                        if last:
                            ins.then_inc(v_lo_done, 1)
                y = y_of(at, 2)
                if y is not None:
                    v, g = y // G, y % G
                    last = y % (UB * G) == UB * G - 1
                    wait(dve, at, z_done, UB * G, y + 1)
                    if last:
                        wait(dve, at, rstd_done, 3, 3 * (y // (UB * G)))
                    dve.bn_stats(stats[:, g, v % UB, :], z_sb[:, v % UB, g, :])
                    if last:
                        dve.drain()
                        for g in range(G):
                            ins = dve.bn_aggr(mean_var[:, g, :], stats[:, g, :, :])
                        ins.then_inc(aggregated, 1)
                v = masked_of(at)
                if v is not None:
                    wait(dve, at, mask_loaded[v % 4], UB // 4, v // 4 + 1, 16)
                    wait(dve, at, scored, SB, (v - 1) * SU)
                    dve.tensor_scalar(masked[v % 2][:, :], mask[v % 4][:, :], 0.0, 0.0, ALU.is_gt, ALU.is_equal) \
                       .then_inc(masked_done, 1)

            all_steps(dve, step)

        @block.tensor
        def _(pe):
            pe.wait_ge(consts_ready, 4 + len(NEG_PARTS))
            for k, m in enumerate(W_ORDER):
                pe.wait_ge(w_loaded[k], 16)
                for co in range(G):
                    for ci in range(G):
                        block_of = slice((co * G + ci) * P, (co * G + ci + 1) * P)
                        ins = nc.tensor.transpose((s_bank + t_bank)[k][:, block_of],
                                                  w_rows[:, m * G + co, ci * P:(ci + 1) * P], ident[:, :])
                ins.then_inc(w_turned, 1)
            pe.wait_ge(w_copied, 4)
            pe.wait_ge(b_loaded, 32)
            for co in range(G):
                for ci in range(G):
                    ins = nc.tensor.matmul(o_bank[0][:, co:co + 1], w_t[:, w_block(3, co, ci), :],
                                           b_in_col[:, 2 * G + ci:2 * G + ci + 1], start=ci == 0, stop=ci == G - 1)
            ins.then_inc(y_bias_psum, 1)
            pe.wait_ge(w_split, 4)
            pe.wait_ge(y_bias_ready, 1)

            def project(dst, matrix, co, hi, lo):
                passes = [(w, a) for w, a in ((w_hi, hi), (w_lo, hi), (w_hi, lo))]
                for k, (w, a) in enumerate(passes):
                    for ci in range(G):
                        ins = nc.tensor.matmul(dst, w[:, w_block(matrix, co, ci), :], a[:, ci, :],
                                               start=k == 0 and ci == 0, stop=k == 2 and ci == G - 1)
                return ins

            def step(at):
                r = scores_of(at)
                if r is not None:
                    v, q = r // SU, r % SU
                    if q == 0:
                        wait(pe, at, q_lo_done, UB * G, (v + 1) * G)
                        wait(pe, at, k_spread[v % 2], UB // 2, v // 2 + 1, 16 * 4 * G)
                        wait(pe, at, masked_done, UB, v + 1)
                    wait(pe, at, shifted, SB, r - 1)
                    cols = masked[v % 2][:, q * STEP:(q + 1) * STEP].rearrange("p (c t) -> p c t", t=CHUNK)
                    nc.tensor.matmul(
                        s_bank[r % 2][:, :].rearrange("p (c a t) -> p c a t", c=2, t=CHUNK), neg_w[:, :],
                        cols.unsqueeze(2).to_broadcast([P, 2, 4, CHUNK]),
                        start=True, stop=False, skip_group_check=True)
                    for c in range(2):
                        chunk = 2 * q + c
                        for g in range(G):
                            dst = s_bank[r % 2][:, (c * G + g) * P:(c * G + g + 1) * P]
                            for k, (a, b) in enumerate(((HI, HI), (HI, LO), (LO, HI))):
                                ins = nc.tensor.matmul(
                                    dst, q_sb[v % 2][:, a, g, chunk, :],
                                    k_sb[v % 2][:, g, b, :, chunk * CHUNK:(chunk + 1) * CHUNK],
                                    start=False, stop=k == 2, skip_group_check=True)
                    ins.then_inc(scored, 1)
                r = scores_of(at, 3)
                if r is not None:
                    wait(pe, at, normed, SB, r + 1)
                    if is_last(r - 2):
                        wait(pe, at, pt_hi_done, SB, r - 1)
                    else:
                        wait_pt_lo(pe, at, r - 2)
                    for k in range(4):
                        ins = nc.tensor.transpose(t_bank[r % 2][:, k * P:(k + 1) * P],
                                                  probs[r % 4][:, k * P:(k + 1) * P], ident[:, :])
                    ins.then_inc(turned, 1)
                j = qk_of(at)
                if j is not None:
                    v = j // 4
                    if j % 4 == 0:
                        wait(pe, at, ctx_lo_done, UB * G, (v + 1) * G)
                    if 0 < j % 4 <= G:
                        wait(pe, at, qk_hi_done, SB, j)
                    else:
                        wait(pe, at, q_lo_done, UB * G, v * G + (j % 4 == 3))
                    project(qk_bank[:, :], 1 if j % 4 < G else 0, j % 2, ctx_hi[v % 2], ctx_lo[v % 2]) \
                        .then_inc(qk_proj, 1)
                w = v_of(at)
                if w is not None:
                    v, half = w // 2, w % 2
                    if at.fixed and at.count(SB // 2, w) <= 5:
                        wait(pe, at, v_lo_done, SB // 2, w)
                    else:
                        wait(pe, at, y_masked, UB * G, w - 5)
                    for a in range(2):
                        t0 = 256 * half + P * a
                        dst = vy_bank[:, C * a:C * a + C]
                        for k, (c, m) in enumerate(((ctx_hi, w_hi), (ctx_hi, w_lo), (ctx_lo, w_hi))):
                            for ci in range(G):
                                wv = m[:, w_block(2, 0, ci):w_block(2, 1, ci) + 1:G, :]
                                ins = nc.tensor.matmul(dst.rearrange("p (a c) -> p a c", a=G),
                                                       c[v % 2][:, ci, t0:t0 + P], wv,
                                                       start=k == 0 and ci == 0, stop=k == 2 and ci == G - 1)
                    ins.then_inc(v_proj, 1)
                r = scores_of(at, 4)
                if r is not None:
                    v, q = r // SU, r % SU
                    wait_pt_lo(pe, at, r)
                    if q % 2 == 0:
                        wait(pe, at, v_lo_done, SB // 2, 2 * v + q // 2 + 1)
                        wait(pe, at, o_hi_done, SB // 2, r // 2 - 1)
                    for c in range(2):
                        chunk = 2 * q + c
                        for g in range(G):
                            t0 = (q % 2) * STEP + c * CHUNK
                            dst = o_tile(r // 2)[:, g, t0:t0 + CHUNK]
                            k = 0
                            for low in range(2):
                                pcol = (c * G + g) * P + low * CHUNK
                                vcol = g * 4 * CHUNK + low * CHUNK
                                for part, pt in ((HI, pt_hi), (LO, pt_hi), (HI, pt_lo)):
                                    ins = nc.tensor.matmul(dst, v_sb[v % 2][:, part, chunk, vcol:vcol + P],
                                                           pt[r % 2][:, pcol:pcol + CHUNK],
                                                           start=k == 0, stop=k == 5)
                                    k += 1
                    ins.then_inc(attended, 1)
                y = y_of(at)
                if y is not None:
                    v, g = y // G, y % G
                    wait(pe, at, o_lo_done, SB // 2, 2 * v + 2)
                    if at.fixed:
                        pe.wait_ge(v_lo_done, min(at.count(SB // 2, y + 6), 2 * UNITS))
                        wait(pe, at, y_masked, UB * G, y)
                    else:
                        wait(pe, at, v_lo_done, SB // 2, y + 6)
                    project(vy_bank[:, :], 3, g, o_hi[v % 2], o_lo[v % 2]).then_inc(y_proj, 1)

            all_steps(pe, step)


_INS = ['x', 'ctx_4096', 'mask_Bx1x4096_ff1', 'L0_xattn_W_in', 'L0_xattn_b_in', 'L0_xattn_W_out', 'L0_xattn_b_out']
_OUTS = [((N, C, T), 'float32')]


def kernel(**inputs):
    import numpy as _np
    import concourse.bacc as _bacc
    from concourse import mybir as _mybir
    from concourse.bass_utils import run_bass_kernel_spmd as _run

    nc = _bacc.Bacc("TRN2", target_bir_lowering=False, num_devices=1)
    arrays, args = {}, []
    for name in _INS:
        a = _np.ascontiguousarray(inputs[name])
        arrays[f"in_{name}_dram"] = a
        args.append(nc.dram_tensor(f"in_{name}_dram", a.shape, _mybir.dt.from_np(a.dtype), kind="ExternalInput").ap())
    for i, (shape, dtype) in enumerate(_OUTS):
        dt = _mybir.dt.from_np(_np.dtype(dtype))
        args.append(nc.dram_tensor(f"out_{i}_dram", shape, dt, kind="ExternalOutput").ap())
    build(nc, *args)
    r = _run(nc, [arrays], core_ids=[0])
    got = tuple(r.results[0][f"out_{i}_dram"] for i in range(len(_OUTS)))
    return got[0]
```
